# Optimizing a Trainium2 kernel written in Bass

```python
import numpy as np
import jax
import jax.numpy as jnp

def _softmax(x, axis=-1):
    return jax.nn.softmax(x, axis=axis)

def _gelu(x):
    return jax.nn.gelu(x, approximate=True)

def _silu(x):
    return jax.nn.silu(x)

def _sigmoid(x):
    return jax.nn.sigmoid(x)

def _layernorm(x, axis=-1, eps=1e-05):
    m = jnp.mean(x, axis=axis, keepdims=True)
    v = jnp.var(x, axis=axis, keepdims=True)
    return (x - m) / jnp.sqrt(v + eps)

def _scatter_add(tgt, idx, src, axis=0):
    return tgt.at[idx].add(src)

def _segment_sum(src, seg, n):
    return jax.ops.segment_sum(src, seg, n)
kernel_name = 'mk_conv_attn_hybrid_d2_conv_nchw512_r2_014330'

def setup_inputs(seed: int=0):
    np.random.seed(seed)
    _w = jnp.asarray

    def _rec_inputs():
        import jax
        import jax.numpy as jnp
        _gk = jax.random.key(seed)
        x = -0.0002928 + 1 * jax.random.normal(jax.random.fold_in(_gk, 1), (8, 256, 32, 32), jnp.float32)
        return x
    x = _rec_inputs()

    def _L0_conv_setup():
        import jax, jax.numpy as jnp
        import numpy as np
        ALPHA = 32.0 ** 2
        HEADS = 8
        DIM_HEAD = 32
        EPS = 1e-05

        def _leaky(x):
            return jnp.where(x >= 0, x, 0.1 * x)

        def _cpb_bias(fmap_size, w0, b0, w1, b1, w2, b2):
            pos = jnp.arange(fmap_size)
            gi, gj = jnp.meshgrid(pos, pos, indexing='ij')
            grid = jnp.stack([gi, gj], axis=-1).reshape(-1, 2)
            rel = grid[:, None, :] - grid[None, :, :]
            rel = jnp.sign(rel) * jnp.log(jnp.abs(rel) + 1.0)
            h = _leaky(jnp.einsum('ijc,dc->ijd', rel.astype(jnp.float32), w0) + b0)
            h = _leaky(jnp.einsum('ijc,dc->ijd', h, w1) + b1)
            h = jnp.einsum('ijc,hc->ijh', h, w2) + b2
            return jnp.transpose(h, (2, 0, 1))

        def _stable_softmax(t, alpha=ALPHA):
            t = t / alpha
            t = t - jax.lax.stop_gradient(jnp.max(t, axis=-1, keepdims=True))
            return jax.nn.softmax(t * alpha, axis=-1)
        key = jax.random.key(seed)
        ks = jax.random.split(key, 9)
        B, C, H, W = (8, 256, 32, 32)
        inner = HEADS * DIM_HEAD
        s = 0.05
        return {'x': jax.random.normal(ks[0], (B, C, H, W), jnp.float32), 'gamma': jnp.ones((1, C, 1, 1), jnp.float32), 'w_qkv': jax.random.normal(ks[1], (inner * 3, C), jnp.float32) * s, 'w_out': jax.random.normal(ks[2], (C, inner), jnp.float32) * s, 'cpb_w0': jax.random.normal(ks[3], (64, 2), jnp.float32) * s, 'cpb_b0': jax.random.normal(ks[4], (64,), jnp.float32) * s, 'cpb_w1': jax.random.normal(ks[5], (64, 64), jnp.float32) * s, 'cpb_b1': jax.random.normal(ks[6], (64,), jnp.float32) * s, 'cpb_w2': jax.random.normal(ks[7], (HEADS, 64), jnp.float32) * s, 'cpb_b2': jax.random.normal(ks[8], (HEADS,), jnp.float32) * s}
    _L0_conv_all = _L0_conv_setup()
    _L0_conv_in = {k: v for k, v in _L0_conv_all.items() if k in ('gamma', 'w_qkv', 'w_out', 'cpb_w0', 'cpb_b0', 'cpb_w1', 'cpb_b1', 'cpb_w2', 'cpb_b2')}
    del _L0_conv_all

    def _L1_attn_setup():
        import jax, jax.numpy as jnp
        import numpy as np
        NUM_HEADS = 8
        B, L, D = (4, 512, 256)

        def sinusoidal_embeddings(length, dim, decay_term=10000.0):
            positions = jnp.arange(1 - length, length, dtype=jnp.float32).reshape(-1, 1)
            div_term = jnp.exp(-jnp.arange(0, dim, 2, dtype=jnp.float32) * (np.log(decay_term) / dim))
            return jnp.concatenate([jnp.sin(positions * div_term), jnp.cos(positions * div_term)], axis=1)
        key = jax.random.key(seed)
        k1, k2 = jax.random.split(key)
        x = jax.random.normal(k1, (B, L, D), dtype=jnp.float32)
        W = jax.random.normal(k2, (D, 3 * D), dtype=jnp.float32) * 0.02
        b = jnp.zeros((3 * D,), dtype=jnp.float32)
        return {'x': x, 'W': W, 'b': b}
    _L1_attn_all = _L1_attn_setup()
    _L1_attn_in = {k: v for k, v in _L1_attn_all.items() if k in ('W', 'b')}
    del _L1_attn_all

    def _L1_ffn_setup():
        import jax, jax.numpy as jnp
        import numpy as np
        EPS = 1e-06
        SINKHORN_ITERS = 8
        TEMPERATURE = 1.0
        B, N, D = (4, 4096, 256)
        E, OUT = (8, 256)
        H = 1

        def _sinkhorn(logits):
            t = jnp.log(jnp.clip(logits, EPS)) / TEMPERATURE
            for _ in range(SINKHORN_ITERS):
                t = t - jax.nn.logsumexp(t, axis=-2, keepdims=True)
                t = t - jax.nn.logsumexp(t, axis=-1, keepdims=True)
            return jnp.exp(t)
        key = jax.random.key(seed)
        k1, k2, k3 = jax.random.split(key, 3)
        x = jax.random.normal(k1, (B, N, D), dtype=jnp.float32)
        gate_weight = jax.random.normal(k2, (H, D, E), dtype=jnp.float32)
        experts = jax.random.normal(k3, (E, D, OUT), dtype=jnp.float32) * 0.02
        return {'x': x, 'gate_weight': gate_weight, 'experts': experts}
    _L1_ffn_all = _L1_ffn_setup()
    _L1_ffn_in = {k: v for k, v in _L1_ffn_all.items() if k in ('gate_weight', 'experts')}
    del _L1_ffn_all
    return {'x': x, 'L0_conv_gamma': _L0_conv_in['gamma'], 'L0_conv_w_qkv': _L0_conv_in['w_qkv'], 'L0_conv_w_out': _L0_conv_in['w_out'], 'L0_conv_cpb_w0': _L0_conv_in['cpb_w0'], 'L0_conv_cpb_b0': _L0_conv_in['cpb_b0'], 'L0_conv_cpb_w1': _L0_conv_in['cpb_w1'], 'L0_conv_cpb_b1': _L0_conv_in['cpb_b1'], 'L0_conv_cpb_w2': _L0_conv_in['cpb_w2'], 'L0_conv_cpb_b2': _L0_conv_in['cpb_b2'], 'L1_attn_W': _L1_attn_in['W'], 'L1_attn_b': _L1_attn_in['b'], 'L1_ffn_gate_weight': _L1_ffn_in['gate_weight'], 'L1_ffn_experts': _L1_ffn_in['experts']}

def reference(x, L0_conv_gamma, L0_conv_w_qkv, L0_conv_w_out, L0_conv_cpb_w0, L0_conv_cpb_b0, L0_conv_cpb_w1, L0_conv_cpb_b1, L0_conv_cpb_w2, L0_conv_cpb_b2, L1_attn_W, L1_attn_b, L1_ffn_gate_weight, L1_ffn_experts):
    import jax
    import jax.numpy as jnp

    def _L0_conv_ref(x, gamma, w_qkv, w_out, cpb_w0, cpb_b0, cpb_w1, cpb_b1, cpb_w2, cpb_b2):
        import jax, jax.numpy as jnp
        import numpy as np
        ALPHA = 32.0 ** 2
        HEADS = 8
        DIM_HEAD = 32
        EPS = 1e-05

        def _leaky(x):
            return jnp.where(x >= 0, x, 0.1 * x)

        def _cpb_bias(fmap_size, w0, b0, w1, b1, w2, b2):
            pos = jnp.arange(fmap_size)
            gi, gj = jnp.meshgrid(pos, pos, indexing='ij')
            grid = jnp.stack([gi, gj], axis=-1).reshape(-1, 2)
            rel = grid[:, None, :] - grid[None, :, :]
            rel = jnp.sign(rel) * jnp.log(jnp.abs(rel) + 1.0)
            h = _leaky(jnp.einsum('ijc,dc->ijd', rel.astype(jnp.float32), w0) + b0)
            h = _leaky(jnp.einsum('ijc,dc->ijd', h, w1) + b1)
            h = jnp.einsum('ijc,hc->ijh', h, w2) + b2
            return jnp.transpose(h, (2, 0, 1))

        def _stable_softmax(t, alpha=ALPHA):
            t = t / alpha
            t = t - jax.lax.stop_gradient(jnp.max(t, axis=-1, keepdims=True))
            return jax.nn.softmax(t * alpha, axis=-1)
        B, C, H, W = x.shape
        n = H * W
        scale = DIM_HEAD ** (-0.5)
        residual = x
        mean = jnp.mean(x, axis=1, keepdims=True)
        var = jnp.var(x, axis=1, keepdims=True)
        xn = (x - mean) / jnp.sqrt(var + EPS) * gamma
        xf = xn.reshape(B, C, n)
        qkv = jnp.einsum('oc,bcn->bon', w_qkv, xf)
        q, k, v = jnp.split(qkv, 3, axis=1)
        rs = lambda t: t.reshape(B, HEADS, DIM_HEAD, n)
        q, k, v = (rs(q), rs(k), rs(v))
        sim = jnp.einsum('bhdi,bhdj->bhij', q, k) * scale
        bias = _cpb_bias(H, cpb_w0, cpb_b0, cpb_w1, cpb_b1, cpb_w2, cpb_b2)
        sim = sim + bias[None]
        attn = _stable_softmax(sim)
        out = jnp.einsum('bhij,bhdj->bhdi', attn, v)
        out = out.reshape(B, HEADS * DIM_HEAD, n)
        out = jnp.einsum('oc,bcn->bon', w_out, out).reshape(B, C, H, W)
        return out + residual

    def _L1_attn_ref(x, W, b):
        import jax, jax.numpy as jnp
        import numpy as np
        NUM_HEADS = 8
        B, L, D = (4, 512, 256)

        def sinusoidal_embeddings(length, dim, decay_term=10000.0):
            positions = jnp.arange(1 - length, length, dtype=jnp.float32).reshape(-1, 1)
            div_term = jnp.exp(-jnp.arange(0, dim, 2, dtype=jnp.float32) * (np.log(decay_term) / dim))
            return jnp.concatenate([jnp.sin(positions * div_term), jnp.cos(positions * div_term)], axis=1)
        batch, length, dim = x.shape
        d_head = dim // NUM_HEADS
        proj = jnp.einsum('bld,de->ble', x, W) + b
        proj = proj.reshape(batch, length, NUM_HEADS, 3 * d_head).transpose(0, 2, 1, 3)
        q, k, v = jnp.split(proj, 3, axis=3)
        qk = jnp.einsum('bhqd,bhkd->bhqk', q, k)
        emb_matrix = sinusoidal_embeddings(length, d_head)
        indices = jnp.arange(length)[:, None] - jnp.arange(length) + length - 1
        embeddings = emb_matrix[indices]
        qe = jnp.einsum('bhqd,qkd->bhqk', q, embeddings)
        weights = jax.nn.softmax((qk + qe) / jnp.sqrt(jnp.float32(d_head)), axis=-1)
        output = jnp.einsum('bhqk,bhkd->bhqd', weights, v)
        return output.transpose(0, 2, 1, 3).reshape(batch, length, dim)

    def _L1_ffn_ref(x, gate_weight, experts):
        import jax, jax.numpy as jnp
        import numpy as np
        EPS = 1e-06
        SINKHORN_ITERS = 8
        TEMPERATURE = 1.0
        B, N, D = (4, 4096, 256)
        E, OUT = (8, 256)
        H = 1

        def _sinkhorn(logits):
            t = jnp.log(jnp.clip(logits, EPS)) / TEMPERATURE
            for _ in range(SINKHORN_ITERS):
                t = t - jax.nn.logsumexp(t, axis=-2, keepdims=True)
                t = t - jax.nn.logsumexp(t, axis=-1, keepdims=True)
            return jnp.exp(t)
        b, n, d = x.shape
        e = experts.shape[0]
        m = n // e
        xh = x[:, None, :, :]
        gate_logits = jnp.einsum('bhnd,hde->bhne', xh, gate_weight)
        gates = _sinkhorn(gate_logits)
        g_t = jnp.swapaxes(gates, -1, -2)
        vals, idx = jax.lax.top_k(g_t, m)
        gate_values = jnp.transpose(vals, (2, 0, 1, 3))[..., None]
        routed = jnp.take_along_axis(xh[:, :, None, :, :], idx[..., None], axis=3)
        routed = jnp.transpose(routed, (2, 0, 1, 3, 4))
        expert_w = experts[:, None, :, :]
        outputs = jnp.einsum('ebhmi,ehio->ebhmo', routed, expert_w)
        outputs = outputs * gate_values
        bh_idx = idx.reshape(b, 1, e * m)
        bh_vals = jnp.transpose(outputs, (1, 2, 0, 3, 4)).reshape(b, 1, e * m, outputs.shape[-1])

        def scat(i1, v1):
            return jnp.zeros((n, v1.shape[-1]), dtype=v1.dtype).at[i1].set(v1)
        routed_back = jax.vmap(jax.vmap(scat))(bh_idx, bh_vals)
        return routed_back[:, 0]

    def _gn(v, G=32, eps=1e-05):
        B_, C_, H_, W_ = v.shape
        g = v.reshape(B_, G, C_ // G, H_, W_)
        m = jnp.mean(g, axis=(2, 3, 4), keepdims=True)
        s = jnp.var(g, axis=(2, 3, 4), keepdims=True)
        return ((g - m) / jnp.sqrt(s + eps)).reshape(v.shape)

    def _ln_c(v, eps=1e-06):
        m = jnp.mean(v, axis=1, keepdims=True)
        s = jnp.var(v, axis=1, keepdims=True)
        return (v - m) / jnp.sqrt(s + eps)

    def _ln_t(v, eps=1e-05):
        m = jnp.mean(v, axis=-1, keepdims=True)
        s = jnp.var(v, axis=-1, keepdims=True)
        return (v - m) / jnp.sqrt(s + eps)

    def _to_tokens(v):
        B_, C_, H_, W_ = v.shape
        return v.reshape(B_, C_, H_ * W_).transpose(0, 2, 1)

    def _from_tokens(t, like):
        B_, C_, H_, W_ = like.shape
        return t.transpose(0, 2, 1).reshape(B_, C_, H_, W_)
    x = _L0_conv_ref(x, L0_conv_gamma, L0_conv_w_qkv, L0_conv_w_out, L0_conv_cpb_w0, L0_conv_cpb_b0, L0_conv_cpb_w1, L0_conv_cpb_b1, L0_conv_cpb_w2, L0_conv_cpb_b2)
    t = _to_tokens(x)
    t = t + _L1_attn_ref(_ln_t(t), L1_attn_W, L1_attn_b)
    t = t + _L1_ffn_ref(_ln_t(t), L1_ffn_gate_weight, L1_ffn_experts)
    x = _from_tokens(t, x)
    return x

_drawn_inputs = setup_inputs


def setup_inputs(seed=0):
    import zlib

    import numpy as np

    out = dict(_drawn_inputs(seed))
    spreads = {'L0_conv_gamma': (1.0, 0.6), 'L1_attn_b': (0.0, 0.1)}
    factors = {'L0_conv_cpb_w0': 8.0,
     'L0_conv_cpb_b0': 8.0,
     'L0_conv_cpb_w1': 8.0,
     'L0_conv_cpb_b1': 8.0,
     'L0_conv_cpb_w2': 8.0,
     'L0_conv_cpb_b2': 8.0,
     'L1_attn_W': 3.305}
    for name, (base, spread) in spreads.items():
        noise = np.random.default_rng([zlib.crc32(name.encode()), seed]).standard_normal(out[name].shape)
        drawn = base * np.exp(spread * noise) if base else spread * noise
        out[name] = jnp.asarray(drawn.astype(out[name].dtype))
    for name, factor in factors.items():
        out[name] = (out[name] * factor).astype(out[name].dtype)
    return out
```

```python
import concourse.bass as bass
from concourse import mybir
from contextlib import ExitStack


def build(nc, x, gamma, wqkv, wout, w1q, b1cols, b1v, gatew, experts, relt, cw0, cb0, cw1, cb1, cw2, cb2,
          ident, rot, etab, out):
    F32, F16 = mybir.dt.float32, mybir.dt.float16
    ALU = mybir.AluOpType
    ACT = mybir.ActivationFunctionType
    AX = mybir.AxisListType

    B, C, N = x.shape
    P = 128
    KT = C // P
    NT = N // P
    H, D = 8, C // 8
    G = H * D // P
    HG = H // G
    W = 32
    SIDE = 2 * W - 1
    ROWS = P // W
    ZU = 2 * W - ROWS
    E = gatew.shape[1]
    M = N // E
    WS = 64.0
    QS = float(D) ** -0.5
    CH = 512
    NC = N // CH
    EPS = 1e-5
    GATE_EPS = 1e-6
    SINKHORN = 8
    RC = 7 * SIDE
    NR = SIDE * SIDE // RC
    UN = NT * G
    ST_N = UN * HG
    PRING = 9
    TLAG = HG + 1

    tdram = nc.dram_tensor("bias_table", [H, SIDE * SIDE], F32).ap()
    edram = nc.dram_tensor("rel_embedding_halves", [2 * D, N], F16).ap()
    t_dram = nc.dram_tensor("tokens_after_attention", [B, P, KT, N], F32).ap()
    h_dram = nc.dram_tensor("normed_halves", [B, P, 2, KT, N], F16).ap()

    ctx = ExitStack()
    with ctx:
        def sb(name, shape, dt):
            return ctx.enter_context(nc.sbuf_tensor(name, shape, dt))

        def sem(name):
            return ctx.enter_context(nc.semaphore(name))

        bias = sb("bias", [P, H, ZU * W], F32)
        stacks = sb("stacks", [P, 3, H, N], F16)
        V = sb("V", [P, NT, C], F32)
        ring = sb("ring", [P, PRING, N], F32)
        PTs = sb("PTs", [P, 3, CH], F32)
        X = sb("X", [P, KT, N], F32)
        XH = sb("XH", [P, KT, N], F16)
        XL = sb("XL", [P, KT, N], F16)
        wqkv_p = sb("wqkv_p", [P, 2, KT, 3 * C], F16)
        wout_p = sb("wout_p", [P, 2, KT, C], F16)
        w1_p = sb("w1_p", [P, 2, KT, 4 * C], F16)
        gate_p = sb("gate_p", [P, 2, KT, E], F16)
        rots = sb("rots", [P, 2, N], F32)
        gates = sb("gates", [P, B * NT * E], F32)
        nmax = sb("nmax", [P, 2, ST_N], F32)
        sums = sb("sums", [P, 2, ST_N], F32)
        rsx = sb("rsx", [P, 2, P], F32)
        cb = sb("cb", [P, NT * E], F32)
        idf = sb("idf", [P, P], F32)
        ones = sb("ones", [P, P], F32)
        bvb = sb("bvb", [P, C], F32)
        bcol = sb("bcol", [P, 6], F32)
        eps = sb("eps", [P, 1], F32)
        rbs = sb("rbs", [P, P], F32)
        oF = sb("oF", [P, P], F32)

        flat = ring[:, :, :].rearrange("p a n -> p (a n)")
        XC = flat[:, 0:KT * N].rearrange("p (k n) -> p k n", k=KT)
        SQ = flat[:, KT * N:2 * KT * N].rearrange("p (k n) -> p k n", k=KT)
        R = flat[:, 2 * KT * N:2 * KT * N + N]
        stage = flat[:, 0:6 * N].bitcast(F16).rearrange("p (s n) -> p s n", n=N)
        qf, qsf, kf = (flat[:, (6 + i) * N:(7 + i) * N] for i in range(3))

        PS = ctx.enter_context(nc.psum_tensor("PS", [P, 2, 2 * CH], F32))
        PTp = ctx.enter_context(nc.psum_tensor("PTp", [P, 2, CH], F32))
        PO = ctx.enter_context(nc.psum_tensor("PO", [P, 2, CH], F32))

        zf = bias[:, :, :].rearrange("p h z -> p (h z)")
        rel = zf[0:2, 0:SIDE * SIDE]
        h0 = zf[0:64, SIDE * SIDE:2 * SIDE * SIDE]
        h1 = zf[0:64, 2 * SIDE * SIDE:3 * SIDE * SIDE]
        tab = flat[0:H, 0:SIDE * SIDE]
        e_f = flat[0:D, 4 * N:5 * N]
        e_p = flat[0:D, 5 * N:6 * N].bitcast(F16).rearrange("p (s n) -> p s n", s=2)
        w_st = stacks[:, :, :, :].rearrange("p a h n -> p (a h n)").bitcast(F32)

        WL = []
        off = 0
        for src, dst, cols in ((wqkv, wqkv_p, 3 * C), (wout, wout_p, C), (w1q, w1_p, 4 * C), (gatew, gate_p, E)):
            WL.append((src, dst, w_st[:, off:off + KT * cols].rearrange("p (k n) -> p k n", k=KT)))
            off += KT * cols
        small = w_st[:, off:off + 256]
        c_w0, c_w1, c_w2 = small[0:2, 0:64], small[0:64, 64:128], small[0:64, 128:128 + H]
        c_b0, c_b1, c_b2 = small[0:64, 140:141], small[0:64, 141:142], small[0:H, 142:143]
        gam = small[:, 144:144 + KT]

        with ExitStack() as es:
            def ssem(name):
                return es.enter_context(nc.semaphore(name))
            net_in, w_in, g_in, cst_in, e_in = (ssem(n) for n in ("net_in", "w_in", "g_in", "cst_in", "e_in"))
            net_mm, net_act, net_dve = ssem("net_mm"), ssem("net_act"), ssem("net_dve")
            w_scaled, w_high, w_low = ssem("w_scaled"), ssem("w_high"), ssem("w_low")
            tab_out, e_out, e_high, e_low, bias_in, set_ch = (
                ssem(n) for n in ("tab_out", "e_out", "e_high", "e_low", "bias_in", "set_ch"))
            block = es.enter_context(nc.Block())
            NETL = 3 * NR

            @block.sync
            def _(sp):
                for dst, src in ((rel, relt), (c_w0, cw0), (c_w1, cw1), (c_w2, cw2), (c_b0, cb0), (c_b1, cb1),
                                 (c_b2, cb2)):
                    sp.dma_start(dst, src).then_inc(net_in, 16)
                sp.dma_start(gam, gamma).then_inc(g_in, 16)
                for src, _, st in WL:
                    sp.dma_start(st, src.rearrange("(k p) n -> p k n", p=P)).then_inc(w_in, 16)
                sp.dma_start(e_f, etab).then_inc(e_in, 16)
                sp.dma_start(idf[:], ident).then_inc(cst_in, 16)
                sp.dma_start(rots[:, :, :], rot).then_inc(cst_in, 16)
                sp.dma_start(bcol[:], b1cols).then_inc(cst_in, 16)
                sp.dma_start(bvb[:], b1v.partition_broadcast(P)).then_inc(cst_in, 16)
                sp.wait_ge(e_low, 1)
                for s in range(2):
                    sp.dma_start(edram[s * D:(s + 1) * D, :], e_p[:, s, :]).then_inc(e_out, 16)
                sp.wait_ge(net_act, NETL)
                sp.dma_start(tdram, tab).then_inc(tab_out, 16)
                sp.wait_ge(tab_out, 16)
                for p in range(P):
                    a, i = divmod(p, W)
                    first = (ROWS - 1 - a) * SIDE + W - 1 - i
                    sp.dma_start(bias[p:p + 1, :, :].rearrange("p h (u j) -> p h u j", u=ZU),
                                 bass.AP(tdram.tensor, first, [[SIDE * SIDE, H], [SIDE, ZU], [1, W]]).unsqueeze(0)
                                 ).then_inc(bias_in, 16)
                sp.wait_ge(bias_in, 16 * P)
                sp.wait_ge(e_out, 32)
                sp.wait_ge(cst_in, 64)

            @block.tensor
            def _(pe):
                pe.wait_ge(net_in, 7 * 16)
                for layer, (w_, src, rows) in enumerate(((c_w0, rel, 64), (c_w1, h0, 64), (c_w2, h1, H))):
                    for c in range(NR):
                        n = layer * NR + c
                        if n >= 2:
                            pe.wait_ge(net_act, n - 1)
                        if layer:
                            pe.wait_ge(net_dve, n - NR + 1)
                        nc.tensor.matmul(PS[0:rows, n % 2, 0:RC], w_, src[:, c * RC:(c + 1) * RC],
                                         start=True, stop=True).then_inc(net_mm, 1)

            @block.scalar
            def _(act):
                for layer, (dst, b_, rows) in enumerate(((h0, c_b0, 64), (h1, c_b1, 64), (tab, c_b2, H))):
                    for c in range(NR):
                        n = layer * NR + c
                        act.wait_ge(net_mm, n + 1)
                        nc.scalar.activation(dst[:, c * RC:(c + 1) * RC], PS[0:rows, n % 2, 0:RC], ACT.Identity,
                                             bias=b_).then_inc(net_act, 1)
                act.wait_ge(e_in, 16)
                nc.scalar.copy(e_p[:, 0, :], e_f).then_inc(e_high, 1)
                for n, (_, dst, st) in enumerate(WL):
                    act.wait_ge(w_scaled, KT * (n + 1))
                    nc.scalar.copy(dst[:, 0, :, :], st).then_inc(w_high, 1)

            @block.gpsimd
            def _(pool):
                nc.gpsimd.memset(ones[:], 1.0 / C)
                nc.gpsimd.memset(eps[:], EPS)

            @block.vector
            def _(dve):
                for layer, dst in enumerate((h0, h1)):
                    for c in range(NR):
                        n = layer * NR + c
                        dve.wait_ge(net_act, n + 1)
                        v = dst[:, c * RC:(c + 1) * RC]
                        nc.vector.scalar_tensor_tensor(out=v, in0=v, scalar=0.1, in1=v, op0=ALU.mult,
                                                       op1=ALU.max).then_inc(net_dve, 1)
                dve.wait_ge(g_in, 16)
                dve.wait_ge(w_in, 16 * len(WL))
                for n, (_, dst, st) in enumerate(WL):
                    for k in range(KT):
                        if n == 0:
                            nc.vector.tensor_scalar(st[:, k, :], st[:, k, :], gam[:, k:k + 1], WS, ALU.mult,
                                                    ALU.mult).then_inc(w_scaled, 1)
                        else:
                            nc.vector.tensor_scalar(st[:, k, :], st[:, k, :], WS, None, ALU.mult).then_inc(w_scaled, 1)
                for n, (_, dst, st) in enumerate(WL):
                    dve.wait_ge(w_high, n + 1)
                    nc.vector.tensor_tensor(dst[:, 1, :, :], st, dst[:, 0, :, :], ALU.subtract)
                dve.wait_ge(e_high, 1)
                nc.vector.tensor_tensor(e_p[:, 1, :], e_f, e_p[:, 0, :], ALU.subtract).then_inc(e_low, 1)
                dve.wait_ge(cst_in, 64)
                nc.vector.tensor_scalar(bcol[:, 0:4], bcol[:, 0:4], -QS, None, ALU.mult)

        names = (["mean0", "var0"] + [("qk0", m) for m in range(2 * G)] + [("v0", i) for i in range(2)]
                 + [("att0", i) for i in range(ST_N)] + [("proj", m) for m in range(KT)]
                 + ["mean1", "var1"] + [("qk1", m) for m in range(3 * G)] + [("v1", i) for i in range(2)]
                 + [("att1", i) for i in range(ST_N)] + ["mean2", "var2", "gate"])
        job = {n: i for i, n in enumerate(names)}
        KTU = NT
        LK = UN * KTU
        VT = 2 * CH // C

        sem_names = ("x_in", "full", "xc", "sq", "xn", "xh", "xl", "stg0", "stg1", "stk", "vals",
                     "nmx", "exps", "t_full", "t_ev0", "t_ev1", "pv", "rs", "rb", "rbc", "fin", "res", "x_out",
                     "qf_s", "qs_s", "kf_s", "qh_s", "qph_s", "kh_s", "rot1", "add_s", "std",
                     "dch")
        S = {n: sem(n) for n in sem_names}
        first_sem, last_sem = S[sem_names[0]].num, S[sem_names[-1]].num
        assert last_sem - first_sem == len(sem_names) - 1
        full = S["full"]
        tev = (S["t_ev0"], S["t_ev1"])

        def att_tile(i):
            u = i // HG
            return u, i % HG, u // NT, u % NT

        def read_out(name):
            kind, i = (name, 0) if isinstance(name, str) else name
            layer = int(kind[-1]) if kind[-1].isdigit() else 0
            return {
                "mean": ("xc", KT * (layer + 1)), "var": ("std", layer + 1),
                "qk": ("stg0", i + 1) if layer == 0 else (("qf_s", "qs_s", "kf_s")[i % 3], i // 3 + 1),
                "v": ("vals", 2 * layer + i + 1),
                "att": ("nmx", i + 1) if layer == 0 else ("exps", ST_N + i + 1),
                "proj": ("res", i + 1),
            }[kind.rstrip("012")]

        with nc.Fori(0, B) as b:
            with nc.Block() as block:

                @block.sync
                def _(sp):
                    for k in range(KT):
                        sp.dma_start(X[:, k, :], x[bass.ds(b, 1), k * P:(k + 1) * P, :].rearrange("a p n -> (a p) n")
                                     ).then_inc(S["x_in"], 16)
                    n = 0
                    for m in range(2 * G):
                        sp.wait_ge(S["stg0"], m + 1)
                        for j in range(HG):
                            for r, part in enumerate(((0, 0, 1, 1), (0, 1, 0, 1))[m % 2]):
                                sp.dma_start(stacks[r * D:(r + 1) * D, m % 2, (m // 2) * HG + j, :],
                                             stage[j * D:(j + 1) * D, 2 * m + part, :]).then_inc(S["stk"], 16)
                    sp.wait_ge(full, job[("att0", ST_N - 1)] + 1)
                    for h in range(H):
                        sp.dma_start(stacks[2 * D:4 * D, 1, h, :], edram).then_inc(S["stk"], 16)
                    for g in range(G):
                        for kind in range(3):
                            sp.wait_ge(S["stg1"], 3 * g + kind + 1)
                            for j in range(HG):
                                h = g * HG + j
                                s = 6 * g + 2 * kind
                                if kind < 2:
                                    moves = [(0, 2 * kind, s), (0, 2 * kind + 1, s),
                                             (2, 2 * kind, s + 1), (2, 2 * kind + 1, s + 1)]
                                else:
                                    moves = [(1, 0, s), (1, 1, s + 1)]
                                for st, r, part in moves:
                                    sp.dma_start(stacks[r * D:(r + 1) * D, st, h, :],
                                                 stage[j * D:(j + 1) * D, part, :]).then_inc(S["stk"], 16)
                    sp.wait_ge(S["fin"], 2 * UN)
                    sp.dma_start(t_dram[bass.ds(b, 1)].rearrange("a p k n -> (a p) k n"), X[:, :, :]).then_inc(S["x_out"], 16)
                    sp.wait_ge(S["xh"], 3 * KT)
                    sp.wait_ge(S["xl"], 3 * KT)
                    sp.dma_start(h_dram[bass.ds(b, 1), :, 0].rearrange("a p k n -> (a p) k n"), XH[:, :, :]).then_inc(S["x_out"], 16)
                    sp.dma_start(h_dram[bass.ds(b, 1), :, 1].rearrange("a p k n -> (a p) k n"), XL[:, :, :]).then_inc(S["x_out"], 16)
                    sp.wait_ge(S["x_out"], 48)

                @block.tensor
                def _(pe):
                    def slot(name):
                        n = job[name]
                        if n >= 2:
                            reader, count = read_out(names[n - 2])
                            pe.wait_ge(S[reader], count)
                        return PS[:, n % 2, :]

                    def over_channels(name, src):
                        ps = slot(name)
                        for c in range(NC):
                            for k in range(KT):
                                last = nc.tensor.matmul(ps[:, c * CH:(c + 1) * CH], ones[:], src[:, k, c * CH:(c + 1) * CH],
                                                        start=(k == 0), stop=(k == KT - 1))
                        last.then_inc(full, 1)

                    def project(name, wp, col):
                        ps = slot(name)
                        steps = [(0, XH), (0, XL), (1, XH)]
                        for k in range(KT):
                            for i, (part, src) in enumerate(steps):
                                for c in range(NC):
                                    last = nc.tensor.matmul(ps[:, c * CH:(c + 1) * CH], wp[:, part, k, col:col + P],
                                                            src[:, k, c * CH:(c + 1) * CH],
                                                            start=(k == 0 and i == 0), stop=(k == KT - 1 and i == 2))
                        last.then_inc(full, 1)

                    def values(name, i, wp, col):
                        ps = slot(name)
                        for t in range(VT):
                            tok = slice((i * VT + t) * P, (i * VT + t + 1) * P)
                            n = 0
                            for k in range(KT):
                                for src, part in ((XH, 0), (XH, 1), (XL, 0)):
                                    last = nc.tensor.matmul(ps[:, t * C:(t + 1) * C], src[:, k, tok],
                                                            wp[:, part, k, col:col + C], start=(n == 0), stop=(n == 3 * KT - 1))
                                    n += 1
                        last.then_inc(full, 1)

                    def scores(layer, i):
                        u, j, g, t = att_tile(i)
                        h = g * HG + j
                        ps = slot((f"att{layer}", i))
                        parts = (0,) if layer == 0 else (0, 2)
                        for q in parts:
                            for c in range(NC):
                                last = nc.tensor.matmul(ps[:, c * CH:(c + 1) * CH], stacks[:, q, h, t * P:(t + 1) * P],
                                                        stacks[:, 1, h, c * CH:(c + 1) * CH],
                                                        start=(q == 0), stop=(q == parts[-1]))
                        last.then_inc(full, 1)

                    def transposes(layer, k):
                        u, kt = divmod(k, KTU)
                        kk = layer * LK + k
                        if kt == 0:
                            pe.wait_ge(S["exps"], layer * ST_N + (u + 1) * HG)
                        if kk >= 2:
                            pe.wait_ge(tev[kk % 2], kk // 2)
                        for j in range(HG):
                            last = nc.tensor.transpose(PTp[:, kk % 2, j * P:(j + 1) * P],
                                                       ring[:, (u * HG + j) % PRING, kt * P:(kt + 1) * P], idf[:])
                        last.then_inc(S["t_full"], 1)

                    def weigh(layer, k):
                        u, kt = divmod(k, KTU)
                        g, t = divmod(u, NT)
                        kk = layer * LK + k
                        uu = layer * UN + u
                        if k == 0:
                            pe.wait_ge(S["vals"], 2 * (layer + 1))
                        pe.wait_ge(tev[kk % 2], kk // 2 + 1)
                        if kt == 0 and uu >= 2:
                            pe.wait_ge(S["fin"], uu - 1)
                        for j in range(HG):
                            last = nc.tensor.matmul(PO[j * D:(j + 1) * D, uu % 2, 0:P],
                                                    V[:, kt, (g * HG + j) * D:(g * HG + j + 1) * D],
                                                    PTs[:, kk % 3, j * P:(j + 1) * P],
                                                    start=(kt == 0), stop=(kt == KTU - 1), skip_group_check=True)
                        last.then_inc(S["pv"], 1)

                    def spread(layer, u):
                        uu = layer * UN + u
                        pe.wait_ge(S["rs"], uu + 1)
                        nc.tensor.matmul(PO[:, uu % 2, P:2 * P],
                                         rsx[:, uu % 2, :], idf[:], start=True, stop=True).then_inc(S["rb"], 1)

                    def attention(layer):
                        scores(layer, 0)
                        for s in range(ST_N + TLAG + 1):
                            for k in (2 * (s - TLAG), 2 * (s - TLAG) + 1):
                                if 0 <= k < LK:
                                    transposes(layer, k)
                                if 0 <= k - 1 < LK:
                                    weigh(layer, k - 1)
                                    if k % KTU == 0:
                                        spread(layer, k // KTU - 1)
                            if s + 1 < ST_N:
                                scores(layer, s + 1)

                    def normed(n):
                        pe.wait_ge(S["xh"], KT * n)
                        pe.wait_ge(S["xl"], KT * n)

                    pe.wait_ge(S["x_in"], 16 * KT)
                    over_channels("mean0", X)
                    pe.wait_ge(S["sq"], KT)
                    over_channels("var0", SQ)
                    normed(1)
                    for m in range(2 * G):
                        project(("qk0", m), wqkv_p, (m % 2) * C + (m // 2) * P)
                    for i in range(2):
                        values(("v0", i), i, wqkv_p, 2 * C)
                    pe.wait_ge(S["stk"], 16 * 2 * G * HG * 4)
                    attention(0)
                    pe.wait_ge(S["fin"], UN)
                    for m in range(KT):
                        project(("proj", m), wout_p, m * P)
                    pe.wait_ge(S["res"], KT)
                    over_channels("mean1", X)
                    pe.wait_ge(S["sq"], 2 * KT)
                    over_channels("var1", SQ)
                    normed(2)
                    for m in range(3 * G):
                        project(("qk1", m), w1_p, (m % 3) * C + (m // 3) * P)
                    for i in range(2):
                        values(("v1", i), i, w1_p, 3 * C)
                    pe.wait_ge(S["stk"], 16 * (2 * G * HG * 4 + H + G * HG * 10))
                    attention(1)
                    pe.wait_ge(S["fin"], 2 * UN)
                    over_channels("mean2", X)
                    pe.wait_ge(S["sq"], 3 * KT)
                    over_channels("var2", SQ)
                    normed(3)
                    ps = slot("gate")
                    for t in range(NT):
                        n = 0
                        for k in range(KT):
                            for src, part in ((XH, 0), (XH, 1), (XL, 0)):
                                last = nc.tensor.matmul(ps[:, t * E:(t + 1) * E], src[:, k, t * P:(t + 1) * P],
                                                        gate_p[:, part, k, :], start=(n == 0), stop=(n == 3 * KT - 1))
                                n += 1
                    last.then_inc(full, 1)

                @block.scalar
                def _(act):
                    def squares(n):
                        for k in range(KT):
                            act.wait_ge(S["xc"], n * KT + k + 1)
                            nc.scalar.activation(SQ[:, k, :], XC[:, k, :], ACT.Square).then_inc(S["sq"], 1)
                        j = job[f"var{n}"]
                        act.wait_ge(full, j + 1)
                        nc.scalar.activation(R, PS[:, j % 2, :], ACT.Sqrt, bias=eps[:]).then_inc(S["std"], 1)
                        for k in range(KT):
                            act.wait_ge(S["xn"], n * KT + k + 1)
                            nc.scalar.copy(XH[:, k, :], XC[:, k, :]).then_inc(S["xh"], 1)

                    def exps(layer, i):
                        u, j, g, t = att_tile(i)
                        n = job[(f"att{layer}", i)]
                        act.wait_ge(S["nmx"], layer * ST_N + i + 1)
                        r = ring[:, i % PRING, :]
                        a = layer * ST_N + i
                        if layer == 1 and i >= PRING:
                            act.wait_ge(S["t_full"], layer * LK + KTU * ((i - PRING) // HG + 1))
                        ins = nc.scalar.activation(r, r if layer == 0 else PS[:, n % 2, :], ACT.Exp,
                                                   bias=nmax[:, layer, i:i + 1], scale=-1.0,
                                                   accum_out=sums[:, layer, i:i + 1])
                        ins.then_inc(S["exps"], 1)

                    def copy_out(layer, k):
                        kk = layer * LK + k
                        act.wait_ge(S["t_full"], kk + 1)
                        if kk >= 3:
                            act.wait_ge(S["pv"], kk - 2)
                        nc.scalar.copy(PTs[:, kk % 3, :], PTp[:, kk % 2, :]).then_inc(tev[0], 1)

                    def attention(layer):
                        for s in range(ST_N + TLAG + 1):
                            if 1 <= s <= ST_N:
                                exps(layer, s - 1)
                            k = 2 * (s - TLAG)
                            if 0 <= k < LK:
                                copy_out(layer, k)

                    squares(0)
                    for m in range(2 * G):
                        n = job[("qk0", m)]
                        act.wait_ge(full, n + 1)
                        nc.scalar.activation(stage[:, 2 * m, :], PS[:, n % 2, :], ACT.Copy,
                                             scale=(QS if m % 2 == 0 else 1.0) / WS).then_inc(S["qh_s"], 1)
                    for i in range(2):
                        n = job[("v0", i)]
                        act.wait_ge(full, n + 1)
                        ins = nc.scalar.activation(V[:, i * VT:(i + 1) * VT, :].rearrange("p t c -> p (t c)"),
                                                   PS[:, n % 2, :], ACT.Copy, scale=1.0 / WS)
                        ins.then_inc(S["vals"], 1)
                    attention(0)
                    squares(1)
                    for g in range(G):
                        q, qs, k = (job[("qk1", 3 * g + i)] for i in range(3))
                        act.wait_ge(full, q + 1)
                        if g:
                            act.wait_ge(S["add_s"], g)
                            act.wait_ge(S["stg1"], 3 * (g - 1) + 1)
                        ins = nc.scalar.activation(qf, PS[:, q % 2, :], ACT.Identity, scale=-QS / WS, bias=bcol[:, g:g + 1])
                        ins.then_inc(S["qf_s"], 1)
                        act.wait_ge(full, qs + 1)
                        if g:
                            act.wait_ge(S["stg1"], 3 * (g - 1) + 2)
                        ins = nc.scalar.activation(qsf, PS[:, qs % 2, :], ACT.Identity, scale=-QS / WS,
                                                   bias=bcol[:, 2 + g:3 + g])
                        ins.then_inc(S["qs_s"], 1)
                        act.wait_ge(S["qf_s"], g + 1)
                        nc.scalar.copy(stage[:, 6 * g, :], qf).then_inc(S["qph_s"], 1)
                        act.wait_ge(S["add_s"], g + 1)
                        nc.scalar.copy(stage[:, 6 * g + 2, :], qsf).then_inc(S["qph_s"], 1)
                        act.wait_ge(full, k + 1)
                        ins = nc.scalar.activation(kf, PS[:, k % 2, :], ACT.Identity, scale=1.0 / WS, bias=bcol[:, 4 + g:5 + g])
                        ins.then_inc(S["kf_s"], 1)
                        act.wait_ge(S["kf_s"], g + 1)
                        nc.scalar.copy(stage[:, 6 * g + 4, :], kf).then_inc(S["kh_s"], 1)
                    attention(1)
                    squares(2)

                @block.gpsimd
                def _(pool):
                    def low(n):
                        pool.wait_ge(S["xh"], n * KT + KT)
                        nc.gpsimd.tensor_tensor(XL[:, KT - 1, :], XC[:, KT - 1, :], XH[:, KT - 1, :],
                                                ALU.subtract).then_inc(S["xl"], 1)
                    low(0)
                    low(1)
                    for g in range(G):
                        pool.wait_ge(S["qf_s"], g + 1)
                        if g:
                            pool.wait_ge(S["kh_s"], g)
                            pool.wait_ge(S["stg1"], 3 * g)
                        nc.gpsimd.tensor_tensor(kf, qf, rots[:, 0, :], ALU.mult).then_inc(S["rot1"], 1)
                        pool.wait_ge(S["qs_s"], g + 1)
                        nc.gpsimd.tensor_tensor(qsf, qsf, rots[:, 1, :], ALU.mult).then_inc(S["rot1"], 1)
                    low(2)

                @block.vector
                def _(dve):
                    chain = [0]

                    def link(ins):
                        chain[0] += 1
                        ins.then_inc(S["dch"], 1)
                        dve.wait_ge(S["dch"], chain[0])

                    def norm(n):
                        j = job[f"mean{n}"]
                        dve.wait_ge(full, j + 1)
                        for k in range(KT):
                            ins = nc.vector.tensor_tensor(XC[:, k, :], X[:, k, :], PS[:, j % 2, :], ALU.subtract)
                            ins.then_inc(S["xc"], 1)
                        dve.wait_ge(S["std"], n + 1)
                        link(nc.vector.reciprocal(R, R))
                        for k in range(KT):
                            ins = nc.vector.tensor_tensor(XC[:, k, :], XC[:, k, :], R, ALU.mult)
                            ins.then_inc(S["xn"], 1)
                        for k in range(KT - 1):
                            dve.wait_ge(S["xh"], n * KT + k + 1)
                            nc.vector.tensor_tensor(XL[:, k, :], XC[:, k, :], XH[:, k, :], ALU.subtract).then_inc(S["xl"], 1)

                    def row_max(layer, i):
                        u, j, g, t = att_tile(i)
                        n = job[(f"att{layer}", i)]
                        dve.wait_ge(full, n + 1)
                        if layer == 0:
                            if i >= PRING:
                                dve.wait_ge(S["t_full"], KTU * ((i - PRING) // HG + 1))
                            z = (ZU - W - ROWS * t) * W
                            ins = nc.vector.tensor_tensor_reduce(
                                out=ring[:, i % PRING, :], in0=PS[:, n % 2, :], in1=bias[:, g * HG + j, z:z + N],
                                scale=-1.0, scalar=3.0e38, op0=ALU.add, op1=ALU.min, accum_out=nmax[:, layer, i:i + 1])
                            ins.then_inc(S["nmx"], 1)
                        else:
                            nc.vector.tensor_reduce(nmax[:, layer, i:i + 1], PS[:, n % 2, :], AX.X,
                                                    ALU.min).then_inc(S["nmx"], 1)

                    def copy_out(layer, k):
                        kk = layer * LK + k
                        dve.wait_ge(S["t_full"], kk + 1)
                        if kk >= 3:
                            dve.wait_ge(S["pv"], kk - 2)
                        nc.vector.tensor_copy(PTs[:, kk % 3, :], PTp[:, kk % 2, :]).then_inc(tev[1], 1)

                    def finish(layer, u):
                        g, t = divmod(u, NT)
                        uu = layer * UN + u
                        tok = slice(t * P, (t + 1) * P)
                        dve.wait_ge(S["rb"], uu + 1)
                        ins = nc.vector.tensor_copy(rbs[:], PO[:, uu % 2, P:2 * P])
                        ins.then_inc(S["rbc"], 1)
                        dve.wait_ge(S["rbc"], uu + 1)
                        dve.wait_ge(S["pv"], layer * LK + (u + 1) * KTU)
                        link(nc.vector.tensor_tensor(oF[:], PO[:, uu % 2, 0:P], rbs[:], ALU.mult))
                        if layer == 0:
                            link(nc.vector.tensor_copy(XH[:, g, tok], oF[:]))
                            nc.vector.tensor_tensor(XL[:, g, tok], oF[:], XH[:, g, tok], ALU.subtract).then_inc(S["fin"], 1)
                        else:
                            nc.vector.tensor_tensor(X[:, g, tok], X[:, g, tok], oF[:], ALU.add).then_inc(S["fin"], 1)

                    def attention(layer):
                        for s in range(ST_N + TLAG + 2):
                            if s < ST_N:
                                row_max(layer, s)
                            if s >= TLAG and (s - TLAG) % HG == 0 and (s - TLAG) // HG < UN:
                                u = (s - TLAG) // HG
                                dve.wait_ge(S["exps"], layer * ST_N + (u + 1) * HG)
                                uu = layer * UN + u
                                if uu >= 2:
                                    dve.wait_ge(S["rb"], uu - 1)
                                nc.vector.reciprocal(
                                    rsx[:, uu % 2, :].rearrange("p (j d) -> p j d", j=HG),
                                    sums[:, layer, u * HG:(u + 1) * HG].unsqueeze(2).broadcast_to([P, HG, D])
                                ).then_inc(S["rs"], 1)
                            k = 2 * (s - TLAG) + 1
                            if 0 <= k < LK:
                                copy_out(layer, k)
                            v = s - 2 * HG - 2
                            if v >= 0 and v % HG == 0:
                                finish(layer, v // HG)
                        for u in range((ST_N + TLAG + 1 - 2 * HG - 2) // HG + 1, UN):
                            finish(layer, u)

                    norm(0)
                    for m in range(2 * G):
                        n = job[("qk0", m)]
                        dve.wait_ge(S["qh_s"], m + 1)
                        ins = nc.vector.scalar_tensor_tensor(out=stage[:, 2 * m + 1, :], in0=PS[:, n % 2, :],
                                                             scalar=(QS if m % 2 == 0 else 1.0) / WS,
                                                             in1=stage[:, 2 * m, :], op0=ALU.mult, op1=ALU.subtract)
                        ins.then_inc(S["stg0"], 1)
                    attention(0)
                    for m in range(KT):
                        n = job[("proj", m)]
                        dve.wait_ge(full, n + 1)
                        ins = nc.vector.scalar_tensor_tensor(out=X[:, m, :], in0=PS[:, n % 2, :], scalar=1.0 / WS,
                                                             in1=X[:, m, :], op0=ALU.mult, op1=ALU.add)
                        ins.then_inc(S["res"], 1)
                    norm(1)
                    for g in range(G):
                        dve.wait_ge(S["qph_s"], 2 * g + 1)
                        ins = nc.vector.tensor_tensor(stage[:, 6 * g + 1, :], qf, stage[:, 6 * g, :], ALU.subtract)
                        ins.then_inc(S["stg1"], 1)
                        dve.wait_ge(S["rot1"], 2 * g + 2)
                        nc.vector.tensor_tensor(qsf, kf, qsf, ALU.add).then_inc(S["add_s"], 1)
                        dve.wait_ge(S["qph_s"], 2 * g + 2)
                        ins = nc.vector.tensor_tensor(stage[:, 6 * g + 3, :], qsf, stage[:, 6 * g + 2, :], ALU.subtract)
                        ins.then_inc(S["stg1"], 1)
                        dve.wait_ge(S["kh_s"], g + 1)
                        nc.vector.tensor_tensor(stage[:, 6 * g + 5, :], kf, stage[:, 6 * g + 4, :],
                                                ALU.subtract).then_inc(S["stg1"], 1)
                    for i in range(2):
                        n = job[("v1", i)]
                        dve.wait_ge(full, n + 1)
                        ins = nc.vector.scalar_tensor_tensor(
                            out=V[:, i * VT:(i + 1) * VT, :], in0=PS[:, n % 2, :].rearrange("p (t c) -> p t c", t=VT),
                            scalar=1.0 / WS, in1=bvb[:].unsqueeze(1).broadcast_to([P, VT, C]), op0=ALU.mult, op1=ALU.add)
                        ins.then_inc(S["vals"], 1)
                    attention(1)
                    norm(2)
                    n = job["gate"]
                    dve.wait_ge(full, n + 1)
                    nc.vector.tensor_scalar(gates[:, bass.ds(b * (NT * E), NT * E)], PS[:, n % 2, 0:NT * E], 1.0 / WS,
                                            GATE_EPS, ALU.mult, ALU.max)

            nc.sync.sem_clear(range(first_sem, last_sem + 1))
            nc.all_engine_barrier()

        BE = B * E
        g4 = gates[:].rearrange("p (b t e) -> p b t e", b=B, t=NT)
        sc = ring[:, :, :].rearrange("p a n -> p (a n)")
        part = sc[:, 0:BE]
        rcp = sc[:, BE:2 * BE]
        gT = sc[0:BE, N:2 * N]
        gW = sc[0:BE, 2 * N:3 * N]
        top = sc[0:BE, 3 * N:3 * N + 8]
        mask = sc[:, 4 * N:4 * N + NT * BE]
        m4 = mask.rearrange("p (t b e) -> p b t e", t=NT, b=B)
        coef = sc[:, 5 * N:5 * N + NT * BE]
        c4 = coef.rearrange("p (b t e) -> p b t e", b=B, t=NT)
        left = sc[:, 6 * N:6 * N + B * NT].rearrange("p (b t) -> p b t", b=B)
        tmp = sc[:, 7 * N:7 * N + B * NT].rearrange("p (b t) -> p b t", b=B)

        gT_src = sc[:, 8 * N:8 * N + NT * BE].rearrange("p (t c) -> p t c", t=NT)

        zf16 = zf.bitcast(F16)
        ex_p = zf16[:, 0:2 * KT * E * C].rearrange("p (s k n) -> p s k n", s=2, k=KT)
        ex_f = w_st[:, 0:KT * E * C].rearrange("p (k n) -> p k n", k=KT)

        with ExitStack() as es:
            def ssem(name):
                return es.enter_context(nc.semaphore(name))
            prt, tot, g_t, g_w, m_t, ch, ex_in, ex_s, ex_h, coef_done = (
                ssem(n) for n in ("prt", "tot", "g_t", "g_w", "m_t", "ch", "ex_in", "ex_s", "ex_h", "coef_done"))
            block = es.enter_context(nc.Block())

            @block.sync
            def _(sp):
                for k in range(KT):
                    sp.dma_start(ex_f[:, k, :].rearrange("p (e o) -> p e o", e=E),
                                 experts[:, k * P:(k + 1) * P, :].rearrange("e p o -> p e o")).then_inc(ex_in, 16)

            @block.scalar
            def _(act):
                for k in range(KT):
                    act.wait_ge(ex_in, 16 * KT)
                    nc.scalar.mul(ex_f[:, k, :], ex_f[:, k, :], WS).then_inc(ex_s, 1)
                for k in range(KT):
                    act.wait_ge(ex_s, k + 1)
                    nc.scalar.copy(ex_p[:, 0, k, :], ex_f[:, k, :]).then_inc(ex_h, 1)

            @block.gpsimd
            def _(pool):
                for k in range(KT):
                    pool.wait_ge(ex_h, k + 1)
                    nc.gpsimd.tensor_tensor(ex_p[:, 1, k, :], ex_f[:, k, :], ex_p[:, 0, k, :], ALU.subtract)

            @block.tensor
            def _(pe):
                for n in range(SINKHORN):
                    pe.wait_ge(prt, n + 1)
                    nc.tensor.matmul(PO[:, 0, 0:BE], ones[:], part, start=True, stop=True).then_inc(tot, 1)
                pe.wait_ge(g_t, 1)
                for t in range(NT):
                    last = nc.tensor.transpose(PS[0:BE, 0, t * P:(t + 1) * P], gT_src[:, t, :], idf[:])
                last.then_inc(m_t, 1)
                pe.wait_ge(g_w, 1)
                for t in range(NT):
                    last = nc.tensor.transpose(PTp[:, 0, t * BE:(t + 1) * BE], gW[:, t * P:(t + 1) * P], idf[0:BE, 0:BE])
                last.then_inc(m_t, 1)

            @block.vector
            def _(dve):
                chain = [0]

                def link(ins):
                    chain[0] += 1
                    ins.then_inc(ch, 1)
                    dve.wait_ge(ch, chain[0])

                p3 = part.rearrange("p (b e) -> p b e", b=B)
                r3 = rcp.rearrange("p (b e) -> p b e", b=B)
                rt = rcp.rearrange("p (b t) -> p b t", b=B)
                pt3 = part.rearrange("p (b t) -> p b t", b=B)
                for n in range(SINKHORN):
                    ins = nc.vector.reduce_sum(p3, g4.rearrange("p b t e -> p b e t"), AX.X)
                    ins.then_inc(prt, 1)
                    dve.wait_ge(tot, n + 1)
                    link(nc.vector.tensor_scalar(rcp, PO[:, 0, 0:BE], float(C), None, ALU.mult))
                    link(nc.vector.reciprocal(rcp, rcp))
                    link(nc.vector.tensor_tensor(g4, g4, r3.unsqueeze(2).broadcast_to([P, B, NT, E]), ALU.mult))
                    link(nc.vector.reduce_sum(pt3, g4, AX.X))
                    link(nc.vector.reciprocal(rt, pt3))
                    link(nc.vector.tensor_tensor(g4, g4, rt.unsqueeze(3).broadcast_to([P, B, NT, E]), ALU.mult))
                nc.vector.tensor_copy(gT_src.rearrange("p t (b e) -> p t b e", b=B),
                                      g4.rearrange("p b t e -> p t b e")).then_inc(g_t, 1)
                dve.wait_ge(m_t, 1)
                link(nc.vector.tensor_copy(gW, PS[0:BE, 0, :]))
                for r in range(M // 8):
                    link(nc.vector.max(top, gW))
                    link(nc.vector.match_replace(gW, top, gW, -1.0))
                ins = nc.vector.tensor_scalar(gW, gW, 0.0, None, ALU.is_lt)
                ins.then_inc(g_w, 1)
                dve.wait_ge(m_t, 2)
                link(nc.vector.tensor_copy(mask, PTp[:, 0, :]))
                link(nc.vector.memset(left, 1.0))
                for e in reversed(range(E)):
                    link(nc.vector.tensor_tensor(tmp, m4[:, :, :, e], left, ALU.mult))
                    link(nc.vector.tensor_tensor(left, left, tmp, ALU.subtract))
                    link(nc.vector.tensor_tensor(c4[:, :, :, e], tmp, g4[:, :, :, e], ALU.mult))

        fb = stacks[:, :, :, :].rearrange("p a h n -> p (a h n)")
        hb = [fb[:, i * 2 * KT * N:(i + 1) * 2 * KT * N].rearrange("p (s k n) -> p s k n", s=2, k=KT) for i in range(1)]
        HB = hb[0]
        TB = X
        cb = cb[:, :]
        acc = flat[:, 0:2 * C].rearrange("p (s c) -> p s c", s=2)
        EJ = 2 * CH // C
        NJ = E // EJ

        fsem = [sem(n) for n in ("f_in", "f_full", "f_ch", "f_acc", "f_t", "f_x", "f_out")]
        f_in, f_full, f_ch, f_acc, f_t, f_x, f_out = fsem
        with nc.Fori(0, B) as b:
            with nc.Block() as block:

                @block.sync
                def _(sp):
                    sp.dma_start(HB[:, :, :, :], h_dram[bass.ds(b, 1)].rearrange("a p s k n -> (a p) s k n")).then_inc(f_in, 16)
                    sp.dma_start(TB[:, :, :], t_dram[bass.ds(b, 1)].rearrange("a p k n -> (a p) k n")).then_inc(f_in, 16)
                    sp.wait_ge(f_x, NT)
                    for k in range(KT):
                        sp.dma_start(out[bass.ds(b, 1), k * P:(k + 1) * P, :].rearrange("a p n -> (a p) n"),
                                     TB[:, k, :]).then_inc(f_out, 16)
                    sp.wait_ge(f_out, 16 * KT)

                @block.tensor
                def _(pe):
                    def back(t):
                        pe.wait_ge(f_acc, (t + 1) * E)
                        if t >= 2:
                            pe.wait_ge(f_x, t - 1)
                        for k in range(KT):
                            last = nc.tensor.transpose(PTp[:, t % 2, k * P:(k + 1) * P], acc[:, t % 2, k * P:(k + 1) * P], idf[:])
                        last.then_inc(f_t, 1)

                    pe.wait_ge(f_in, 32)
                    for t in range(NT):
                        for q in range(NJ):
                            n = t * NJ + q
                            if n >= 2:
                                pe.wait_ge(f_acc, (n - 1) * EJ)
                            for c in range(2):
                                i = 0
                                for k in range(KT):
                                    for s, w in ((0, 0), (0, 1), (1, 0)):
                                        last = nc.tensor.matmul(
                                            PS[:, n % 2, c * CH:(c + 1) * CH], HB[:, s, k, t * P:(t + 1) * P],
                                            ex_p[:, w, k, (2 * q + c) * CH:(2 * q + c + 1) * CH],
                                            start=(i == 0), stop=(i == 3 * KT - 1))
                                        i += 1
                            last.then_inc(f_full, 1)
                            if q == NJ - 1 and t >= 1:
                                back(t - 1)
                    back(NT - 1)

                @block.vector
                def _(dve):
                    chain = [0]

                    def link(ins):
                        chain[0] += 1
                        ins.then_inc(f_ch, 1)
                        dve.wait_ge(f_ch, chain[0])

                    def add_back(t):
                        dve.wait_ge(f_t, t + 1)
                        ins = nc.vector.tensor_tensor(TB[:, :, t * P:(t + 1) * P], TB[:, :, t * P:(t + 1) * P],
                                                      PTp[:, t % 2, 0:C].rearrange("p (k n) -> p k n", k=KT), ALU.add)
                        ins.then_inc(f_x, 1)

                    link(nc.vector.tensor_scalar(cb, coef[:, bass.ds(b * (NT * E), NT * E)], 1.0 / WS, None, ALU.mult))
                    dve.wait_ge(f_in, 32)
                    for t in range(NT):
                        for e in range(E):
                            n = (t * E + e) // EJ
                            if e % EJ == 0:
                                dve.wait_ge(f_full, n + 1)
                            if e == 0 and t >= 2:
                                dve.wait_ge(f_t, t - 1)
                            ps = PS[:, n % 2, (e % EJ) * C:(e % EJ + 1) * C]
                            c_e = cb[:, t * E + e:t * E + e + 1]
                            if e == 0:
                                ins = nc.vector.tensor_scalar(acc[:, t % 2, :], ps, c_e, None, ALU.mult)
                            else:
                                ins = nc.vector.scalar_tensor_tensor(out=acc[:, t % 2, :], in0=ps, scalar=c_e,
                                                                     in1=acc[:, t % 2, :], op0=ALU.mult, op1=ALU.add)
                            ins.then_inc(f_acc, 1)
                            if e < E - 1:
                                dve.wait_ge(f_acc, t * E + e + 1)
                        if t >= 1:
                            add_back(t - 1)
                    add_back(NT - 1)

            nc.sync.sem_clear(range(fsem[0].num, fsem[-1].num + 1))
            nc.all_engine_barrier()


def kernel(**inputs):
    import numpy as np
    import concourse.bacc as _bacc
    from concourse import mybir as _mybir
    from concourse.bass_utils import run_bass_kernel_spmd as _run

    a = {k: np.asarray(v) for k, v in inputs.items()}
    B, C, HH, WW = a["x"].shape
    N, H = HH * WW, 8
    D = C // H
    con = np.ascontiguousarray
    wqkv = con(a["L0_conv_w_qkv"].T)
    wout = con(a["L0_conv_w_out"].T)
    w1 = a["L1_attn_W"].reshape(C, H, 3, D)
    b1 = a["L1_attn_b"].reshape(H, 3, D)
    swap = np.concatenate([np.arange(D // 2, D), np.arange(D // 2)])
    w1q = con(np.concatenate([w1[:, :, 0].reshape(C, C), w1[:, :, 0][:, :, swap].reshape(C, C),
                              w1[:, :, 1].reshape(C, C), w1[:, :, 2].reshape(C, C)], axis=1))
    cols = [b1[:, 0].reshape(-1, 128), b1[:, 0][:, swap].reshape(-1, 128), b1[:, 1].reshape(-1, 128)]
    b1cols = con(np.concatenate(cols, axis=0).T)
    b1v = con(b1[:, 2].reshape(-1))
    r = np.arange(-(WW - 1), WW, dtype=np.float32)
    lr = (-np.sign(r) * np.log(np.abs(r) + np.float32(1.0))).astype(np.float32)
    relt = con(np.stack([np.repeat(lr, len(r)), np.tile(lr, len(r))]))
    div = np.exp(-np.arange(0, D, 2, dtype=np.float32) * np.float32(np.log(10000.0) / D)).astype(np.float64)
    ang = div[:, None] * np.arange(N)[None, :]
    s, c = np.sin(ang), np.cos(ang)
    rot = np.stack([np.tile(np.concatenate([s, s]), (128 // D, 1)), np.tile(np.concatenate([c, -c]), (128 // D, 1))],
                   axis=1).astype(np.float32)
    etab = np.concatenate([c, s]).astype(np.float32)
    data = {
        "x": con(a["x"].reshape(B, C, N)),
        "gamma": con(a["L0_conv_gamma"].reshape(-1, 128).T),
        "wqkv": wqkv, "wout": wout, "w1q": w1q, "b1cols": b1cols, "b1v": b1v,
        "gatew": con(a["L1_ffn_gate_weight"][0]), "experts": con(a["L1_ffn_experts"]),
        "relt": relt,
        "cw0": con(a["L0_conv_cpb_w0"].T), "cb0": con(a["L0_conv_cpb_b0"][:, None]),
        "cw1": con(a["L0_conv_cpb_w1"].T), "cb1": con(a["L0_conv_cpb_b1"][:, None]),
        "cw2": con(a["L0_conv_cpb_w2"].T), "cb2": con(a["L0_conv_cpb_b2"][:, None]),
        "ident": np.eye(128, dtype=np.float32), "rot": con(rot), "etab": con(etab),
    }
    nc = _bacc.Bacc("TRN2", target_bir_lowering=False, num_devices=1)
    args = {k: nc.dram_tensor(f"in_{k}", list(v.shape), _mybir.dt.from_np(v.dtype), kind="ExternalInput").ap()
            for k, v in data.items()}
    out = nc.dram_tensor("out_0", [B, C, N], _mybir.dt.float32, kind="ExternalOutput").ap()
    build(nc, **args, out=out)
    res = _run(nc, [{f"in_{k}": v for k, v in data.items()}], core_ids=[0])
    return res.results[0]["out_0"].reshape(B, C, HH, WW)
```

```python
import concourse.bass as bass
from concourse import mybir
from contextlib import ExitStack


def build(nc, x, gamma, wqkv, wout, w1q, b1cols, b1v, gatew, experts, relt, cw0, cb0, cw1, cb1, cw2, cb2,
          ident, rot, etab, out):
    F32, F16 = mybir.dt.float32, mybir.dt.float16
    ALU = mybir.AluOpType
    ACT = mybir.ActivationFunctionType
    AX = mybir.AxisListType

    B, C, N = x.shape
    P = 128
    KT = C // P
    NT = N // P
    H, D = 8, C // 8
    G = H * D // P
    HG = H // G
    W = 32
    SIDE = 2 * W - 1
    ROWS = P // W
    ZU = 2 * W - ROWS
    E = gatew.shape[1]
    M = N // E
    WS = 64.0
    QS = float(D) ** -0.5
    CH = 512
    NC = N // CH
    EPS = 1e-5
    GATE_EPS = 1e-6
    SINKHORN = 8
    RC = 7 * SIDE
    NR = SIDE * SIDE // RC
    UN = NT * G
    ST_N = UN * HG
    PRING = 9
    NB = 2
    KTU = NT
    TLAG = HG + 1

    tdram = nc.dram_tensor("bias_table", [H, SIDE * SIDE], F32).ap()
    edram = nc.dram_tensor("rel_embedding_halves", [2 * D, N], F16).ap()
    qk_dram = [nc.dram_tensor(f"query_key_halves_{i}", [B, G, (4, 6)[i], P, N], F16).ap() for i in range(2)]
    v_dram = [nc.dram_tensor(f"values_{i}", [B, P, NT, C], F32).ap() for i in range(2)]
    o_dram = nc.dram_tensor("attended_halves", [B, P, 2, KT, N], F16).ap()
    x1_dram = nc.dram_tensor("tokens_after_first", [B, P, KT, N], F32).ap()
    t_dram = nc.dram_tensor("tokens_after_attention", [B, P, KT, N], F32).ap()
    h_dram = nc.dram_tensor("normed_halves", [B, P, 2, KT, N], F16).ap()

    ctx = ExitStack()
    with ctx:
        def sb(name, shape, dt):
            return ctx.enter_context(nc.sbuf_tensor(name, shape, dt))

        def sem(name):
            return ctx.enter_context(nc.semaphore(name))

        wqkv_p = sb("wqkv_p", [P, 2, KT, 3 * C], F16)
        wout_p = sb("wout_p", [P, 2, KT, C], F16)
        w1_p = sb("w1_p", [P, 2, KT, 4 * C], F16)
        gate_p = sb("gate_p", [P, 2, KT, E], F16)
        gates = sb("gates", [P, B * NT * E], F32)
        idf = sb("idf", [P, P], F32)
        ones = sb("ones", [P, P], F32)
        bvb = sb("bvb", [P, C], F32)
        bcol = sb("bcol", [P, 6], F32)
        eps = sb("eps", [P, 1], F32)
        bias = sb("bias", [P, H, ZU * W], F32)
        zf = bias[:, :, :].rearrange("p h z -> p (h z)")

        PS = ctx.enter_context(nc.psum_tensor("PS", [P, 8, CH], F32))

        def reset(sems):
            nums = sorted(s.num for s in sems)
            first = [n for n in nums if n - 1 not in nums]
            for a, b in zip(first, [n for n in nums if n + 1 not in nums]):
                nc.sync.sem_clear(range(a, b + 1))
            nc.all_engine_barrier()

        with ExitStack() as es:
            def ssem(name):
                return es.enter_context(nc.semaphore(name))

            w_sum = KT * (3 * C + C + 4 * C + E)
            flat = es.enter_context(nc.sbuf_tensor("set_scratch", [P, 6 * N], F32))
            w_st = es.enter_context(nc.sbuf_tensor("set_weights", [P, w_sum + 256], F32))
            rel = zf[0:2, 0:SIDE * SIDE]
            h0 = zf[0:64, SIDE * SIDE:2 * SIDE * SIDE]
            h1 = zf[0:64, 2 * SIDE * SIDE:3 * SIDE * SIDE]
            tab = flat[0:H, 0:SIDE * SIDE]
            e_f = flat[0:D, 4 * N:5 * N]
            e_p = flat[0:D, 5 * N:6 * N].bitcast(F16).rearrange("p (s n) -> p s n", s=2)

            WL = []
            off = 0
            for src, dst, cols in ((wqkv, wqkv_p, 3 * C), (wout, wout_p, C), (w1q, w1_p, 4 * C), (gatew, gate_p, E)):
                WL.append((src, dst, w_st[:, off:off + KT * cols].rearrange("p (k n) -> p k n", k=KT)))
                off += KT * cols
            small = w_st[:, off:off + 256]
            c_w0, c_w1, c_w2 = small[0:2, 0:64], small[0:64, 64:128], small[0:64, 128:128 + H]
            c_b0, c_b1, c_b2 = small[0:64, 140:141], small[0:64, 141:142], small[0:H, 142:143]
            gam = small[:, 144:144 + KT]

            net_in, w_in, g_in, cst_in, e_in = (ssem(n) for n in ("net_in", "w_in", "g_in", "cst_in", "e_in"))
            net_mm, net_act, net_dve = ssem("net_mm"), ssem("net_act"), ssem("net_dve")
            w_scaled, w_high, w_low = ssem("w_scaled"), ssem("w_high"), ssem("w_low")
            tab_out, e_out, e_high, e_low, bias_in, set_ch = (
                ssem(n) for n in ("tab_out", "e_out", "e_high", "e_low", "bias_in", "set_ch"))
            blk = ExitStack()
            block = blk.enter_context(nc.Block())
            NETL = 3 * NR

            @block.sync
            def _(sp):
                for dst, src in ((rel, relt), (c_w0, cw0), (c_w1, cw1), (c_w2, cw2), (c_b0, cb0), (c_b1, cb1),
                                 (c_b2, cb2)):
                    sp.dma_start(dst, src).then_inc(net_in, 16)
                sp.dma_start(gam, gamma).then_inc(g_in, 16)
                for src, _, st in WL:
                    sp.dma_start(st, src.rearrange("(k p) n -> p k n", p=P)).then_inc(w_in, 16)
                sp.dma_start(e_f, etab).then_inc(e_in, 16)
                sp.dma_start(idf[:], ident).then_inc(cst_in, 16)
                sp.dma_start(bcol[:], b1cols).then_inc(cst_in, 16)
                sp.dma_start(bvb[:], b1v.partition_broadcast(P)).then_inc(cst_in, 16)
                sp.wait_ge(e_low, 1)
                for s in range(2):
                    sp.dma_start(edram[s * D:(s + 1) * D, :], e_p[:, s, :]).then_inc(e_out, 16)
                sp.wait_ge(net_act, NETL)
                sp.dma_start(tdram, tab).then_inc(tab_out, 16)
                sp.wait_ge(tab_out, 16)
                for p in range(P):
                    a, i = divmod(p, W)
                    first = (ROWS - 1 - a) * SIDE + W - 1 - i
                    sp.dma_start(bias[p:p + 1, :, :].rearrange("p h (u j) -> p h u j", u=ZU),
                                 bass.AP(tdram.tensor, first, [[SIDE * SIDE, H], [SIDE, ZU], [1, W]]).unsqueeze(0)
                                 ).then_inc(bias_in, 16)
                sp.wait_ge(bias_in, 16 * P)
                sp.wait_ge(e_out, 32)
                sp.wait_ge(cst_in, 48)

            @block.tensor
            def _(pe):
                pe.wait_ge(net_in, 7 * 16)
                for layer, (w_, src, rows) in enumerate(((c_w0, rel, 64), (c_w1, h0, 64), (c_w2, h1, H))):
                    for c in range(NR):
                        n = layer * NR + c
                        if n >= 4:
                            pe.wait_ge(net_act, n - 3)
                        if layer:
                            pe.wait_ge(net_dve, n - NR + 1)
                        nc.tensor.matmul(PS[0:rows, n % 4, 0:RC], w_, src[:, c * RC:(c + 1) * RC],
                                         start=True, stop=True).then_inc(net_mm, 1)

            @block.scalar
            def _(act):
                for layer, (dst, b_, rows) in enumerate(((h0, c_b0, 64), (h1, c_b1, 64), (tab, c_b2, H))):
                    for c in range(NR):
                        n = layer * NR + c
                        act.wait_ge(net_mm, n + 1)
                        nc.scalar.activation(dst[:, c * RC:(c + 1) * RC], PS[0:rows, n % 4, 0:RC], ACT.Identity,
                                             bias=b_).then_inc(net_act, 1)
                act.wait_ge(e_in, 16)
                nc.scalar.copy(e_p[:, 0, :], e_f).then_inc(e_high, 1)
                for n, (_, dst, st) in enumerate(WL):
                    act.wait_ge(w_scaled, KT * (n + 1))
                    nc.scalar.copy(dst[:, 0, :, :], st).then_inc(w_high, 1)

            @block.gpsimd
            def _(pool):
                nc.gpsimd.memset(ones[:], 1.0 / C)
                nc.gpsimd.memset(eps[:], EPS)

            @block.vector
            def _(dve):
                for layer, dst in enumerate((h0, h1)):
                    for c in range(NR):
                        n = layer * NR + c
                        dve.wait_ge(net_act, n + 1)
                        v = dst[:, c * RC:(c + 1) * RC]
                        nc.vector.scalar_tensor_tensor(out=v, in0=v, scalar=0.1, in1=v, op0=ALU.mult,
                                                       op1=ALU.max).then_inc(net_dve, 1)
                dve.wait_ge(g_in, 16)
                dve.wait_ge(w_in, 16 * len(WL))
                for n, (_, dst, st) in enumerate(WL):
                    for k in range(KT):
                        if n == 0:
                            nc.vector.tensor_scalar(st[:, k, :], st[:, k, :], gam[:, k:k + 1], WS, ALU.mult,
                                                    ALU.mult).then_inc(w_scaled, 1)
                        else:
                            nc.vector.tensor_scalar(st[:, k, :], st[:, k, :], WS, None, ALU.mult).then_inc(w_scaled, 1)
                for n, (_, dst, st) in enumerate(WL):
                    dve.wait_ge(w_high, n + 1)
                    nc.vector.tensor_tensor(dst[:, 1, :, :], st, dst[:, 0, :, :], ALU.subtract)
                dve.wait_ge(e_high, 1)
                nc.vector.tensor_tensor(e_p[:, 1, :], e_f, e_p[:, 0, :], ALU.subtract).then_inc(e_low, 1)
                dve.wait_ge(cst_in, 48)
                nc.vector.tensor_scalar(bcol[:, 0:4], bcol[:, 0:4], -QS, None, ALU.mult)

            blk.close()
            reset([net_in, w_in, g_in, cst_in, e_in, net_mm, net_act, net_dve, w_scaled, w_high, w_low, tab_out, e_out,
                   e_high, e_low, bias_in, set_ch])

        def batch(dram, b):
            return dram[bass.ds(b, 1)]

        TB_ = 4
        NCH = TB_ * NC
        TT = CH // P

        def token_phase(kind):
            with ExitStack() as es:
                def ssem(name):
                    return es.enter_context(nc.semaphore(f"{name}_{kind}"))

                def tile(name, shape, dt):
                    return es.enter_context(nc.sbuf_tensor(f"{name}_{kind}", shape, dt))

                NQ = (2 * G, 3 * G, 0)[kind]
                NV = (2, 2, 0)[kind]
                NP = (0, KT, 0)[kind]
                STG = (4, 6, 0)[kind]
                wp = (wqkv_p, w1_p, gate_p)[kind]
                XR = 4
                xin = tile("xin", [P, XR, KT, CH], F32)
                xc = tile("xc", [P, 3, KT, CH], F32)
                sq = tile("sq", [P, 2, KT, CH], F32)
                rstd = tile("rstd", [P, 2, CH], F32)
                xh = tile("xh", [P, 3, KT, CH], F16)
                xl = tile("xl", [P, 3, KT, CH], F16)
                if kind < 2:
                    stg = tile("stg", [P, 2, G, STG, CH], F16)
                    vst = tile("vst", [P, 2, TT, C], F32)
                if kind == 1:
                    oin = tile("oin", [P, 2, 2, KT, CH], F16)
                    rots = tile("rots", [P, 2, N], F32)
                    qf = tile("qf", [P, 2, CH], F32)
                    qsf = tile("qsf", [P, 2, CH], F32)
                    rf = tile("rf", [P, 2, CH], F32)
                    kf = tile("kf", [P, 2, CH], F32)

                sems = [ssem(n) for n in ("full", "res", "centred", "squared", "std", "rstd_ok",
                                          "scaled", "high", "low", "q_high", "kf_ok", "qf_ok", "qs_ok", "turned",
                                          "added", "k_high", "q_low", "vals", "gated", "rot_in")]
                (full, res, centred, squared, std, rstd_ok, scaled, high, low, q_high, kf_ok,
                 qf_ok, qs_ok, turned, added, k_high, q_low, vals, gated, rot_in) = sems
                SR = 3 if kind == 2 else 2
                loaded, o_loaded, stored, v_stored, x_stored = (
                    [ssem(f"{n}{i}") for i in range(XR)] for n in ("loaded", "o_loaded", "stored", "v_stored", "x_stored"))
                sems += loaded + o_loaded + stored + v_stored + x_stored

                def x_loaded(u):
                    return loaded[u % XR], 16 * (u // XR + 1)

                def is_stored(u):
                    return stored[u % SR], 32 * (u // SR + 1)

                order = []
                for u in range(-3, NCH):
                    n_, w_ = u + 3, u + 2
                    a = [("proj", n_, m) for m in range(NP)] if n_ < NCH else []
                    first = [("qk", u, m) for m in range(NQ // 2)] if u >= 0 else []
                    mean = [("mean", n_, 0)] if n_ < NCH else []
                    second = [("qk", u, m) for m in range(NQ // 2, NQ)] if u >= 0 else []
                    var = [("var", w_, 0)] if 0 <= w_ < NCH else []
                    v = [("v", u, m) for m in range(NV)] if u >= 0 else []
                    g_ = [("gate", u, 0)] if kind == 2 and u >= 0 else []
                    order += a + first + mean + second + var + v + g_
                at = {n: i for i, n in enumerate(order)}

                def read_out(name):
                    what, u, m = name
                    if what == "qk":
                        if kind == 0:
                            return q_low, u * NQ + m + 1
                        return (qf_ok, qs_ok, kf_ok)[m % 3], u * G + m // 3 + 1
                    return {"proj": (res, KT * u + m + 1), "mean": (centred, KT * (u + 1)), "var": (std, u + 1),
                            "v": (vals, NV * u + m + 1), "gate": (gated, u + 1)}[what]

                def bank(name):
                    return PS[:, at[name] % 8, :]

                def last_use(u):
                    if kind == 2:
                        return is_stored(u)
                    return full, at[("v", u, NV - 1)] + 1

                with nc.Fori(0, B // TB_) as i:
                    with nc.Block() as block:

                        def where(u):
                            return i * TB_ + u // NC, slice((u % NC) * CH, (u % NC + 1) * CH)

                        @block.sync
                        def _(sp):
                            def load(u):
                                b, tok = where(u)
                                if u >= XR:
                                    sp.wait_ge(centred, KT * (u - XR + 1))
                                if kind == 1:
                                    if u >= XR:
                                        sp.wait_ge(x_stored[u % XR], 16 * (u // XR))
                                    if u >= 2:
                                        sp.wait_ge(full, at[("proj", u - 2, KT - 1)] + 1)
                                    sp.dma_start(oin[:, u % 2], batch(o_dram, b)[:, :, :, :, tok].rearrange(
                                        "a p s k n -> (a p) s k n")).then_inc(o_loaded[u % 2], 16)
                                if kind < 2:
                                    src = batch(x, b)[:, :, tok].rearrange("a (k p) n -> (a p) k n", p=P)
                                else:
                                    src = batch(t_dram, b)[:, :, :, tok].rearrange("a p k n -> (a p) k n")
                                sp.dma_start(xin[:, u % XR], src).then_inc(loaded[u % XR], 16)

                            def store(u):
                                b, tok = where(u)
                                if kind == 2:
                                    sp.wait_ge(high, KT * (u + 1))
                                    sp.wait_ge(low, KT * (u + 1))
                                    for s, t_ in enumerate((xh, xl)):
                                        sp.dma_start(batch(h_dram, b)[:, :, s, :, tok].rearrange("a p k n -> (a p) k n"),
                                                     t_[:, u % 3]).then_inc(stored[u % SR], 16)
                                    return
                                for g in range(G):
                                    sp.wait_ge(q_low, (u * G + g + 1) * (STG // 2))
                                    sp.dma_start(batch(qk_dram[kind], b)[:, g, :, :, tok].rearrange("a s p n -> (a p) s n"),
                                                 stg[:, u % 2, g]).then_inc(stored[u % SR], 16)
                                sp.wait_ge(vals, NV * (u + 1))
                                sp.dma_start(batch(v_dram[kind], b)[:, :, (u % NC) * TT:(u % NC + 1) * TT].rearrange(
                                    "a p t c -> (a p) t c"), vst[:, u % 2]).then_inc(v_stored[u % 2], 16)

                            if kind == 1:
                                sp.dma_start(rots[:, :, :], rot).then_inc(rot_in, 16)
                            first = XR if kind != 1 else 2
                            for u in range(first):
                                load(u)
                            for u in range(-3, NCH):
                                if kind == 1 and u + 3 < NCH:
                                    b, tok = where(u + 3)
                                    sp.wait_ge(res, KT * (u + 4))
                                    sp.dma_start(batch(x1_dram, b)[:, :, :, tok].rearrange("a p k n -> (a p) k n"),
                                                 xin[:, (u + 3) % XR]).then_inc(x_stored[(u + 3) % XR], 16)
                                if first <= u + 3 + first < NCH:
                                    load(u + 3 + first)
                                if u >= 0:
                                    store(u)
                            for u in range(NCH - XR, NCH):
                                if u >= NCH - SR:
                                    sp.wait_ge(*is_stored(u))
                                if kind < 2 and u >= NCH - 2:
                                    sp.wait_ge(v_stored[u % 2], 16 * (u // 2 + 1))
                                if kind == 1:
                                    sp.wait_ge(x_stored[u % XR], 16 * (u // XR + 1))

                        @block.tensor
                        def _(pe):
                            def product(u, out, wts, col, halves):
                                n = 0
                                for k in range(KT):
                                    for part, s in ((0, 0), (0, 1), (1, 0)):
                                        last = nc.tensor.matmul(out, wts[:, part, k, col:col + P], halves(s, k),
                                                                start=(n == 0), stop=(n == 3 * KT - 1))
                                        n += 1
                                return last

                            def tokens_first(u, out, tok, wts, col, cols):
                                n = 0
                                for k in range(KT):
                                    for src, part in ((xh, 0), (xh, 1), (xl, 0)):
                                        last = nc.tensor.matmul(out, src[:, u % 3, k, tok], wts[:, part, k, col:col + cols],
                                                                start=(n == 0), stop=(n == 3 * KT - 1))
                                        n += 1
                                return last

                            normed = set()
                            for name in order:
                                what, u, m = name
                                n = at[name]
                                if n >= 8:
                                    reader, count = read_out(order[n - 8])
                                    pe.wait_ge(reader, count)
                                if what in ("qk", "v", "gate") and u not in normed:
                                    normed.add(u)
                                    pe.wait_ge(high, KT * (u + 1))
                                    pe.wait_ge(low, KT * (u + 1))
                                ps = bank(name)
                                if what == "proj":
                                    pe.wait_ge(o_loaded[u % 2], 16 * (u // 2 + 1))
                                    last = product(u, ps, wout_p, m * P, lambda s, k: oin[:, u % 2, s, k, :])
                                elif what in ("mean", "var"):
                                    if what == "mean":
                                        pe.wait_ge(*((res, KT * (u + 1)) if kind == 1 else x_loaded(u)))
                                        src = xin[:, u % XR]
                                    else:
                                        pe.wait_ge(squared, KT * (u + 1))
                                        src = sq[:, u % 2]
                                    for k in range(KT):
                                        last = nc.tensor.matmul(ps, ones[:], src[:, k, :], start=(k == 0), stop=(k == KT - 1))
                                elif what == "qk":
                                    col = (m % 2) * C + (m // 2) * P if kind == 0 else (m % 3) * C + (m // 3) * P
                                    last = product(u, ps, wp, col, lambda s, k: (xh, xl)[s][:, u % 3, k, :])
                                elif what == "v":
                                    for t in range(2):
                                        last = tokens_first(u, ps[:, t * C:(t + 1) * C],
                                                            slice((2 * m + t) * P, (2 * m + t + 1) * P), wp,
                                                            (2 + kind) * C, C)
                                else:
                                    for t in range(TT):
                                        last = tokens_first(u, ps[:, t * E:(t + 1) * E], slice(t * P, (t + 1) * P),
                                                            gate_p, 0, E)
                                last.then_inc(full, 1)

                        @block.scalar
                        def _(act):
                            def stage_free(u):
                                if u >= 2:
                                    act.wait_ge(*is_stored(u - 2))

                            for name in order:
                                what, u, m = name
                                n = at[name]
                                if what == "mean":
                                    for k in range(KT):
                                        act.wait_ge(centred, KT * u + k + 1)
                                        if u >= 2:
                                            act.wait_ge(full, at[("var", u - 2, 0)] + 1)
                                        nc.scalar.activation(sq[:, u % 2, k, :], xc[:, u % 3, k, :],
                                                             ACT.Square).then_inc(squared, 1)
                                elif what == "var":
                                    act.wait_ge(full, n + 1)
                                    if u >= 2:
                                        act.wait_ge(scaled, KT * (u - 1))
                                    nc.scalar.activation(rstd[:, u % 2, :], bank(name), ACT.Sqrt, bias=eps[:]).then_inc(std, 1)
                                elif what == "qk" and kind == 0:
                                    act.wait_ge(full, n + 1)
                                    stage_free(u)
                                    nc.scalar.activation(stg[:, u % 2, m // 2, 2 * (m % 2), :], bank(name), ACT.Copy,
                                                         scale=(QS if m % 2 == 0 else 1.0) / WS).then_inc(q_high, 1)
                                elif what == "qk":
                                    g, w = divmod(m, 3)
                                    s = u * G + g
                                    if m == 0:
                                        stage_free(u)
                                    act.wait_ge(full, n + 1)
                                    if w == 0:
                                        if s >= 2:
                                            act.wait_ge(q_low, 3 * (s - 2) + 1)
                                            act.wait_ge(turned, 2 * (s - 2) + 1)
                                        nc.scalar.activation(qf[:, s % 2, :], bank(name), ACT.Identity, scale=-QS / WS,
                                                             bias=bcol[:, g:g + 1]).then_inc(qf_ok, 1)
                                        act.wait_ge(qf_ok, s + 1)
                                        nc.scalar.copy(stg[:, u % 2, g, 0, :], qf[:, s % 2, :]).then_inc(q_high, 1)
                                    elif w == 1:
                                        if s >= 2:
                                            act.wait_ge(q_low, 3 * (s - 2) + 2)
                                        nc.scalar.activation(qsf[:, s % 2, :], bank(name), ACT.Identity, scale=-QS / WS,
                                                             bias=bcol[:, 2 + g:3 + g]).then_inc(qs_ok, 1)
                                    else:
                                        if s >= 2:
                                            act.wait_ge(q_low, 3 * (s - 2) + 3)
                                        nc.scalar.activation(kf[:, s % 2, :], bank(name), ACT.Identity, scale=1.0 / WS,
                                                             bias=bcol[:, 4 + g:5 + g]).then_inc(kf_ok, 1)
                                        act.wait_ge(kf_ok, s + 1)
                                        nc.scalar.copy(stg[:, u % 2, g, 4, :], kf[:, s % 2, :]).then_inc(k_high, 1)
                                        act.wait_ge(added, s + 1)
                                        nc.scalar.copy(stg[:, u % 2, g, 2, :], qsf[:, s % 2, :]).then_inc(q_high, 1)
                                elif what == "v" and kind == 0:
                                    act.wait_ge(full, n + 1)
                                    if u >= 2:
                                        act.wait_ge(v_stored[u % 2], 16 * (u // 2))
                                    nc.scalar.activation(vst[:, u % 2, 2 * m:2 * m + 2, :].rearrange("p t c -> p (t c)"),
                                                         bank(name), ACT.Copy, scale=1.0 / WS).then_inc(vals, 1)
                                if what == "var":
                                    for k in range(KT):
                                        act.wait_ge(scaled, KT * u + k + 1)
                                        if u >= 3 and k == 0:
                                            act.wait_ge(*last_use(u - 3))
                                        nc.scalar.copy(xh[:, u % 3, k, :], xc[:, u % 3, k, :]).then_inc(high, 1)

                        @block.gpsimd
                        def _(pool):
                            if kind != 1:
                                return
                            pool.wait_ge(rot_in, 16)
                            for s in range(NCH * G):
                                u = s // G
                                tok = slice((u % NC) * CH, (u % NC + 1) * CH)
                                pool.wait_ge(qf_ok, s + 1)
                                if s >= 2:
                                    pool.wait_ge(added, s - 1)
                                nc.gpsimd.tensor_tensor(rf[:, s % 2, :], qf[:, s % 2, :], rots[:, 0, tok],
                                                        ALU.mult).then_inc(turned, 1)
                                pool.wait_ge(qs_ok, s + 1)
                                nc.gpsimd.tensor_tensor(qsf[:, s % 2, :], qsf[:, s % 2, :], rots[:, 1, tok],
                                                        ALU.mult).then_inc(turned, 1)

                        @block.vector
                        def _(dve):
                            for name in order:
                                what, u, m = name
                                n = at[name]
                                if what == "proj":
                                    dve.wait_ge(full, n + 1)
                                    dve.wait_ge(*x_loaded(u))
                                    nc.vector.scalar_tensor_tensor(out=xin[:, u % XR, m, :], in0=bank(name), scalar=1.0 / WS,
                                                                   in1=xin[:, u % XR, m, :], op0=ALU.mult,
                                                                   op1=ALU.add).then_inc(res, 1)
                                elif what == "mean":
                                    dve.wait_ge(full, n + 1)
                                    dve.wait_ge(*((res, KT * (u + 1)) if kind == 1 else x_loaded(u)))
                                    if u >= 3:
                                        dve.wait_ge(high, KT * (u - 2))
                                        dve.wait_ge(low, KT * (u - 2))
                                    for k in range(KT):
                                        nc.vector.tensor_tensor(xc[:, u % 3, k, :], xin[:, u % XR, k, :], bank(name),
                                                                ALU.subtract).then_inc(centred, 1)
                                elif what == "var":
                                    dve.wait_ge(std, u + 1)
                                    nc.vector.reciprocal(rstd[:, u % 2, :], rstd[:, u % 2, :]).then_inc(rstd_ok, 1)
                                    dve.wait_ge(rstd_ok, u + 1)
                                    for k in range(KT):
                                        dve.wait_ge(squared, KT * u + k + 1)
                                        nc.vector.tensor_tensor(xc[:, u % 3, k, :], xc[:, u % 3, k, :], rstd[:, u % 2, :],
                                                                ALU.mult).then_inc(scaled, 1)
                                    if u >= 3:
                                        dve.wait_ge(*last_use(u - 3))
                                    for k in range(KT):
                                        dve.wait_ge(high, KT * u + k + 1)
                                        nc.vector.tensor_tensor(xl[:, u % 3, k, :], xc[:, u % 3, k, :], xh[:, u % 3, k, :],
                                                                ALU.subtract).then_inc(low, 1)
                                elif what == "qk" and kind == 0:
                                    dve.wait_ge(q_high, u * NQ + m + 1)
                                    s = stg[:, u % 2, m // 2]
                                    nc.vector.scalar_tensor_tensor(
                                        out=s[:, 2 * (m % 2) + 1, :], in0=bank(name), scalar=(QS if m % 2 == 0 else 1.0) / WS,
                                        in1=s[:, 2 * (m % 2), :], op0=ALU.mult, op1=ALU.subtract).then_inc(q_low, 1)
                                elif what == "qk":
                                    g, w = divmod(m, 3)
                                    s = u * G + g
                                    if w == 0:
                                        dve.wait_ge(q_high, 2 * s + 1)
                                        nc.vector.tensor_tensor(stg[:, u % 2, g, 1, :], qf[:, s % 2, :], stg[:, u % 2, g, 0, :],
                                                                ALU.subtract).then_inc(q_low, 1)
                                    elif w == 2:
                                        dve.wait_ge(turned, 2 * (s + 1))
                                        nc.vector.tensor_tensor(qsf[:, s % 2, :], rf[:, s % 2, :], qsf[:, s % 2, :],
                                                                ALU.add).then_inc(added, 1)
                                        dve.wait_ge(q_high, 2 * s + 2)
                                        nc.vector.tensor_tensor(stg[:, u % 2, g, 3, :], qsf[:, s % 2, :], stg[:, u % 2, g, 2, :],
                                                                ALU.subtract).then_inc(q_low, 1)
                                        dve.wait_ge(k_high, s + 1)
                                        nc.vector.tensor_tensor(stg[:, u % 2, g, 5, :], kf[:, s % 2, :], stg[:, u % 2, g, 4, :],
                                                                ALU.subtract).then_inc(q_low, 1)
                                elif what == "v" and kind == 1:
                                    dve.wait_ge(full, n + 1)
                                    if u >= 2:
                                        dve.wait_ge(v_stored[u % 2], 16 * (u // 2))
                                    nc.vector.scalar_tensor_tensor(
                                        out=vst[:, u % 2, 2 * m:2 * m + 2, :], in0=bank(name).rearrange("p (t c) -> p t c", t=2),
                                        scalar=1.0 / WS, in1=bvb[:].unsqueeze(1).broadcast_to([P, 2, C]), op0=ALU.mult,
                                        op1=ALU.add).then_inc(vals, 1)
                                elif what == "gate":
                                    dve.wait_ge(full, n + 1)
                                    b, tok = where(u)
                                    nc.vector.tensor_scalar(
                                        gates[:, bass.ds(b * (NT * E) + (u % NC) * TT * E, TT * E)], bank(name)[:, 0:TT * E],
                                        1.0 / WS, GATE_EPS, ALU.mult, ALU.max).then_inc(gated, 1)

                    reset(sems)

        def attention_phase(layer):
            with ExitStack() as es:
                def ssem(name):
                    return es.enter_context(nc.semaphore(f"{name}_a{layer}"))

                def tile(name, shape, dt):
                    return es.enter_context(nc.sbuf_tensor(f"{name}_a{layer}", shape, dt))

                NS = (2, 3)[layer]
                stacks = tile("stacks", [P, 2, NS, HG, N], F16)
                V = tile("V", [P, NB, NT, C], F32)
                ring = tile("ring", [P, PRING, N], F32)
                PTs = tile("PTs", [P, 3, CH], F32)
                nmax = tile("nmax", [P, NB * ST_N], F32)
                sums = tile("sums", [P, NB * ST_N], F32)
                rsum = tile("rsum", [P, 2, HG], F32)
                rsx = tile("rsx", [P, 2, P], F32)
                rbs = tile("rbs", [P, 2, P], F32)
                oF = tile("oF", [P, 2, P], F32)
                if layer == 0:
                    res_ = tile("res", [P, NB, 2, KT, N], F16)
                else:
                    res_ = tile("res", [P, NB, KT, N], F32)
                scores_ps = [PS[:, 2 * i:2 * i + 2, :].rearrange("p a n -> p (a n)") for i in range(2)]
                turned_ps = [PS[:, 4 + i, :] for i in range(2)]
                out_ps = [PS[:, 6 + i, :] for i in range(2)]

                NU = NB * UN
                NTL = NU * HG
                LK = NU * KTU
                NG = NB * G
                TG = NT * HG
                LOADS = 16 * (8 if layer == 0 else 10)

                sems = [ssem(n) for n in ("stk0", "stk1", "v_in0", "v_in1", "x_in", "full", "nmx", "exps", "t_full", "ev_act", "ev_dve",
                                          "weighed", "rs1", "rs", "spread", "rb_copy", "of", "fin", "hi", "out_st")]
                (stk0, stk1, v_in0, v_in1, x_in, full, nmx, exps, t_full, ev_act, ev_dve, weighed, rs1, rs, spread_, rb_copy, of, fin,
                 hi, out_st) = sems
                tev, v_in, stk = (ev_act, ev_dve), (v_in0, v_in1), (stk0, stk1)

                def place(i):
                    u = i // HG
                    return u, i % HG, u // UN, (u // NT) % G, u % NT

                def load_group(sp, q, b, g):
                    src = batch(qk_dram[layer], b)[:, g].rearrange("a s (j d) n -> d (a s) j n", d=D)
                    if layer == 0:
                        moves = [(r, 0, s) for r, s in enumerate((0, 0, 1, 1))] + [(r, 1, 2 + s) for r, s in enumerate((0, 1, 0, 1))]
                    else:
                        moves = ([(r, 0, s) for r, s in enumerate((0, 0, 2, 2))] + [(0, 1, 4), (1, 1, 5)]
                                 + [(r, 2, s) for r, s in enumerate((1, 1, 3, 3))])
                    for r, st, s in moves:
                        sp.dma_start(stacks[r * D:(r + 1) * D, q % 2, st], src[:, s]).then_inc(stk[q % 2], 16)

                def load_values(sp, slot, b):
                    sp.dma_start(V[:, slot], batch(v_dram[layer], b).rearrange("a p t c -> (a p) t c")).then_inc(v_in[slot], 16)

                with nc.Block() as block:
                    @block.sync
                    def _(sp):
                        if layer == 1:
                            for q in range(2):
                                for j in range(HG):
                                    sp.dma_start(stacks[2 * D:4 * D, q, 1, j, :], edram).then_inc(x_in, 16)
                            sp.wait_ge(x_in, 16 * 2 * HG)
                        load_group(sp, 0, 0, 0)
                        load_values(sp, 0, 0)
                        sp.wait_ge(stk0, LOADS)
                        sp.wait_ge(v_in0, 16)
                reset(sems)

                with nc.Fori(0, B // NB) as i_:
                    with nc.Block() as block:

                        @block.sync
                        def _(sp):
                            b0 = i_ * NB
                            if layer == 1:
                                for s in range(NB):
                                    sp.dma_start(res_[:, s], batch(x1_dram, b0 + s).rearrange("a p k n -> (a p) k n")).then_inc(x_in, 16)
                            load_group(sp, 1, b0, 1)
                            load_values(sp, 1, b0 + 1)
                            for q in range(2, NG + 1):
                                sp.wait_ge(full, (q - 1) * TG)
                                load_group(sp, q, (b0 + q // G) % B, q % G)
                                if q == G + 1:
                                    sp.wait_ge(weighed, UN * KTU)
                                    load_values(sp, 0, (b0 + NB) % B)
                            for s in range(NB):
                                dst = batch(o_dram if layer == 0 else t_dram, b0 + s)
                                sp.wait_ge(fin, (s + 1) * UN)
                                if layer == 0:
                                    sp.dma_start(dst.rearrange("a p s k n -> (a p) s k n"), res_[:, s]).then_inc(out_st, 16)
                                else:
                                    sp.dma_start(dst.rearrange("a p k n -> (a p) k n"), res_[:, s]).then_inc(out_st, 16)
                            for s in range(2):
                                sp.wait_ge(stk[s], LOADS * (NG // 2))
                            sp.wait_ge(v_in0, 16)
                            sp.wait_ge(v_in1, 16)
                            sp.wait_ge(out_st, 16 * NB)

                        @block.tensor
                        def _(pe):
                            def scores(i):
                                u, j, bb, g, t = place(i)
                                q = i // TG
                                if i % TG == 0 and q >= 1:
                                    pe.wait_ge(stk[q % 2], LOADS * ((q + 1) // 2))
                                if i >= 2:
                                    pe.wait_ge(*((nmx, i - 1) if layer == 0 else (exps, i - 1)))
                                parts = (0,) if layer == 0 else (0, 2)
                                for st in parts:
                                    for c in range(NC):
                                        last = nc.tensor.matmul(scores_ps[i % 2][:, c * CH:(c + 1) * CH],
                                                                stacks[:, q % 2, st, j, t * P:(t + 1) * P],
                                                                stacks[:, q % 2, 1, j, c * CH:(c + 1) * CH],
                                                                start=(st == 0), stop=(st == parts[-1]))
                                last.then_inc(full, 1)

                            def transposes(k):
                                u, kt = divmod(k, KTU)
                                if kt == 0:
                                    pe.wait_ge(exps, (u + 1) * HG)
                                if k >= 2:
                                    pe.wait_ge(tev[k % 2], k // 2)
                                for j in range(HG):
                                    last = nc.tensor.transpose(turned_ps[k % 2][:, j * P:(j + 1) * P],
                                                               ring[:, (u * HG + j) % PRING, kt * P:(kt + 1) * P], idf[:])
                                last.then_inc(t_full, 1)

                            def weigh(k):
                                u, kt = divmod(k, KTU)
                                _, _, bb, g, t = place(u * HG)
                                if k == UN * KTU:
                                    pe.wait_ge(v_in1, 16)
                                pe.wait_ge(tev[k % 2], k // 2 + 1)
                                if kt == 0 and u >= 2:
                                    pe.wait_ge(of, u - 1)
                                for j in range(HG):
                                    last = nc.tensor.matmul(out_ps[u % 2][j * D:(j + 1) * D, 0:P],
                                                            V[:, bb, kt, (g * HG + j) * D:(g * HG + j + 1) * D],
                                                            PTs[:, k % 3, j * P:(j + 1) * P],
                                                            start=(kt == 0), stop=(kt == KTU - 1), skip_group_check=True)
                                last.then_inc(weighed, 1)

                            def spread(u):
                                pe.wait_ge(rs, u + 1)
                                nc.tensor.matmul(out_ps[u % 2][:, P:2 * P], rsx[:, u % 2, :], idf[:], start=True,
                                                 stop=True).then_inc(spread_, 1)

                            scores(0)
                            for s in range(NTL + TLAG + 1):
                                for k in (2 * (s - TLAG), 2 * (s - TLAG) + 1):
                                    if 0 <= k < LK:
                                        transposes(k)
                                    if 0 <= k - 1 < LK:
                                        weigh(k - 1)
                                        if k % KTU == 0:
                                            spread(k // KTU - 1)
                                if s + 1 < NTL:
                                    scores(s + 1)

                        @block.scalar
                        def _(act):
                            def exponentials(i):
                                act.wait_ge(nmx, i + 1)
                                r = ring[:, i % PRING, :]
                                if layer == 1 and i >= PRING:
                                    act.wait_ge(t_full, KTU * ((i - PRING) // HG + 1))
                                nc.scalar.activation(r, r if layer == 0 else scores_ps[i % 2], ACT.Exp,
                                                     bias=nmax[:, i:i + 1], scale=-1.0,
                                                     accum_out=sums[:, i:i + 1]).then_inc(exps, 1)

                            def copy_out(k):
                                act.wait_ge(t_full, k + 1)
                                if k >= 3:
                                    act.wait_ge(weighed, k - 2)
                                nc.scalar.copy(PTs[:, k % 3, :], turned_ps[k % 2]).then_inc(ev_act, 1)

                            def copy_sums(u):
                                act.wait_ge(spread_, u + 1)
                                if u >= 2:
                                    act.wait_ge(of, u - 1)
                                nc.scalar.copy(rbs[:, u % 2, :], out_ps[u % 2][:, P:2 * P]).then_inc(rb_copy, 1)

                            for s in range(NTL + 2 * HG + 3):
                                if 1 <= s <= NTL:
                                    exponentials(s - 1)
                                k = 2 * (s - TLAG)
                                if 0 <= k < LK:
                                    copy_out(k)
                                v = s - 2 * HG - 2
                                if v >= 0 and v % HG == 0 and v // HG < NU:
                                    copy_sums(v // HG)

                        @block.gpsimd
                        def _(pool):
                            if layer == 1:
                                return
                            for u in range(NU):
                                _, _, bb, g, t = place(u * HG)
                                tok = slice(t * P, (t + 1) * P)
                                pool.wait_ge(of, u + 1)
                                nc.gpsimd.tensor_copy(res_[:, bb, 0, g, tok], oF[:, u % 2, :]).then_inc(hi, 1)
                                pool.wait_ge(hi, u + 1)
                                nc.gpsimd.tensor_tensor(res_[:, bb, 1, g, tok], oF[:, u % 2, :], res_[:, bb, 0, g, tok],
                                                        ALU.subtract).then_inc(fin, 1)

                        @block.vector
                        def _(dve):
                            def row_max(i):
                                u, j, bb, g, t = place(i)
                                dve.wait_ge(full, i + 1)
                                if layer == 0:
                                    if i >= PRING:
                                        dve.wait_ge(t_full, KTU * ((i - PRING) // HG + 1))
                                    z = (ZU - W - ROWS * t) * W
                                    nc.vector.tensor_tensor_reduce(
                                        out=ring[:, i % PRING, :], in0=scores_ps[i % 2], in1=bias[:, g * HG + j, z:z + N],
                                        scale=-1.0, scalar=3.0e38, op0=ALU.add, op1=ALU.min,
                                        accum_out=nmax[:, i:i + 1]).then_inc(nmx, 1)
                                else:
                                    nc.vector.tensor_reduce(nmax[:, i:i + 1], scores_ps[i % 2], AX.X,
                                                            ALU.min).then_inc(nmx, 1)

                            def copy_out(k):
                                dve.wait_ge(t_full, k + 1)
                                if k >= 3:
                                    dve.wait_ge(weighed, k - 2)
                                nc.vector.tensor_copy(PTs[:, k % 3, :], turned_ps[k % 2]).then_inc(ev_dve, 1)

                            def reciprocals(u):
                                dve.wait_ge(exps, (u + 1) * HG)
                                nc.vector.reciprocal(rsum[:, u % 2, :], sums[:, u * HG:(u + 1) * HG]).then_inc(rs1, 1)
                                dve.wait_ge(rs1, u + 1)
                                if u >= 2:
                                    dve.wait_ge(spread_, u - 1)
                                nc.vector.tensor_copy(rsx[:, u % 2, :].rearrange("p (j d) -> p j d", j=HG),
                                                      rsum[:, u % 2, :].unsqueeze(2).broadcast_to([P, HG, D])).then_inc(rs, 1)

                            def finish(u):
                                _, _, bb, g, t = place(u * HG)
                                tok = slice(t * P, (t + 1) * P)
                                dve.wait_ge(rb_copy, u + 1)
                                dve.wait_ge(weighed, (u + 1) * KTU)
                                if layer == 0 and u >= 2:
                                    dve.wait_ge(fin, u - 1)
                                nc.vector.tensor_tensor(oF[:, u % 2, :], out_ps[u % 2][:, 0:P], rbs[:, u % 2, :],
                                                        ALU.mult).then_inc(of, 1)
                                if layer == 1:
                                    dve.wait_ge(of, u + 1)
                                    dve.wait_ge(x_in, 16 * NB)
                                    nc.vector.tensor_tensor(res_[:, bb, g, tok], res_[:, bb, g, tok], oF[:, u % 2, :],
                                                            ALU.add).then_inc(fin, 1)

                            for s in range(NTL + 2 * HG + 4):
                                if s < NTL:
                                    row_max(s)
                                if s >= TLAG and (s - TLAG) % HG == 0 and (s - TLAG) // HG < NU:
                                    reciprocals((s - TLAG) // HG)
                                k = 2 * (s - TLAG) + 1
                                if 0 <= k < LK:
                                    copy_out(k)
                                v = s - 2 * HG - 3
                                if v >= 0 and v % HG == 0 and v // HG < NU:
                                    finish(v // HG)

                    reset(sems)

        token_phase(0)
        attention_phase(0)
        token_phase(1)
        attention_phase(1)
        token_phase(2)

        BE = B * E
        g4 = gates[:].rearrange("p (b t e) -> p b t e", b=B, t=NT)
        sc = sb("sink_scratch", [P, 9 * N], F32)[:, :]
        part = sc[:, 0:BE]
        rcp = sc[:, BE:2 * BE]
        gT = sc[0:BE, N:2 * N]
        gW = sc[0:BE, 2 * N:3 * N]
        top = sc[0:BE, 3 * N:3 * N + 8]
        mask = sc[:, 4 * N:4 * N + NT * BE]
        m4 = mask.rearrange("p (t b e) -> p b t e", t=NT, b=B)
        coef = sb("coef", [P, NT * BE], F32)[:, :]
        c4 = coef.rearrange("p (b t e) -> p b t e", b=B, t=NT)
        left = sc[:, 6 * N:6 * N + B * NT].rearrange("p (b t) -> p b t", b=B)
        tmp = sc[:, 7 * N:7 * N + B * NT].rearrange("p (b t) -> p b t", b=B)

        gT_src = sc[:, 8 * N:8 * N + NT * BE].rearrange("p (t c) -> p t c", t=NT)

        zf16 = zf.bitcast(F16)
        ex_p = zf16[:, 0:2 * KT * E * C].rearrange("p (s k n) -> p s k n", s=2, k=KT)
        ex_f = zf[:, KT * E * C:2 * KT * E * C].rearrange("p (k n) -> p k n", k=KT)

        with ExitStack() as es:
            def ssem(name):
                return es.enter_context(nc.semaphore(name))
            prt, tot, g_t, g_w, m_t, ch, ex_in, ex_s, ex_h, coef_done = (
                ssem(n) for n in ("prt", "tot", "g_t", "g_w", "m_t", "ch", "ex_in", "ex_s", "ex_h", "coef_done"))
            blk = ExitStack()
            block = blk.enter_context(nc.Block())

            @block.sync
            def _(sp):
                for k in range(KT):
                    sp.dma_start(ex_f[:, k, :].rearrange("p (e o) -> p e o", e=E),
                                 experts[:, k * P:(k + 1) * P, :].rearrange("e p o -> p e o")).then_inc(ex_in, 16)

            @block.scalar
            def _(act):
                for k in range(KT):
                    act.wait_ge(ex_in, 16 * KT)
                    nc.scalar.mul(ex_f[:, k, :], ex_f[:, k, :], WS).then_inc(ex_s, 1)
                for k in range(KT):
                    act.wait_ge(ex_s, k + 1)
                    nc.scalar.copy(ex_p[:, 0, k, :], ex_f[:, k, :]).then_inc(ex_h, 1)

            @block.gpsimd
            def _(pool):
                for k in range(KT):
                    pool.wait_ge(ex_h, k + 1)
                    nc.gpsimd.tensor_tensor(ex_p[:, 1, k, :], ex_f[:, k, :], ex_p[:, 0, k, :], ALU.subtract)

            @block.tensor
            def _(pe):
                for n in range(SINKHORN):
                    pe.wait_ge(prt, n + 1)
                    nc.tensor.matmul(PS[:, 2, 0:BE], ones[:], part, start=True, stop=True).then_inc(tot, 1)
                pe.wait_ge(g_t, 1)
                for t in range(NT):
                    last = nc.tensor.transpose(PS[0:BE, t // 4, (t % 4) * P:(t % 4 + 1) * P], gT_src[:, t, :], idf[:])
                last.then_inc(m_t, 1)
                pe.wait_ge(g_w, 1)
                for t in range(NT):
                    last = nc.tensor.transpose(PS[:, 3, t * BE:(t + 1) * BE], gW[:, t * P:(t + 1) * P], idf[0:BE, 0:BE])
                last.then_inc(m_t, 1)

            @block.vector
            def _(dve):
                chain = [0]

                def link(ins):
                    chain[0] += 1
                    ins.then_inc(ch, 1)
                    dve.wait_ge(ch, chain[0])

                p3 = part.rearrange("p (b e) -> p b e", b=B)
                r3 = rcp.rearrange("p (b e) -> p b e", b=B)
                rt = rcp.rearrange("p (b t) -> p b t", b=B)
                pt3 = part.rearrange("p (b t) -> p b t", b=B)
                for n in range(SINKHORN):
                    ins = nc.vector.reduce_sum(p3, g4.rearrange("p b t e -> p b e t"), AX.X)
                    ins.then_inc(prt, 1)
                    dve.wait_ge(tot, n + 1)
                    link(nc.vector.tensor_scalar(rcp, PS[:, 2, 0:BE], float(C), None, ALU.mult))
                    link(nc.vector.reciprocal(rcp, rcp))
                    link(nc.vector.tensor_tensor(g4, g4, r3.unsqueeze(2).broadcast_to([P, B, NT, E]), ALU.mult))
                    link(nc.vector.reduce_sum(pt3, g4, AX.X))
                    link(nc.vector.reciprocal(rt, pt3))
                    link(nc.vector.tensor_tensor(g4, g4, rt.unsqueeze(3).broadcast_to([P, B, NT, E]), ALU.mult))
                nc.vector.tensor_copy(gT_src.rearrange("p t (b e) -> p t b e", b=B),
                                      g4.rearrange("p b t e -> p t b e")).then_inc(g_t, 1)
                dve.wait_ge(m_t, 1)
                link(nc.vector.tensor_copy(gW.rearrange("p (a n) -> p a n", a=2), PS[0:BE, 0:2, :]))
                for r in range(M // 8):
                    link(nc.vector.max(top, gW))
                    link(nc.vector.match_replace(gW, top, gW, -1.0))
                ins = nc.vector.tensor_scalar(gW, gW, 0.0, None, ALU.is_lt)
                ins.then_inc(g_w, 1)
                dve.wait_ge(m_t, 2)
                link(nc.vector.tensor_copy(mask, PS[:, 3, :]))
                link(nc.vector.memset(left, 1.0))
                for e in reversed(range(E)):
                    link(nc.vector.tensor_tensor(tmp, m4[:, :, :, e], left, ALU.mult))
                    link(nc.vector.tensor_tensor(left, left, tmp, ALU.subtract))
                    link(nc.vector.tensor_tensor(c4[:, :, :, e], tmp, g4[:, :, :, e], ALU.mult))

            blk.close()
            reset([prt, tot, g_t, g_w, m_t, ch, ex_in, ex_s, ex_h, coef_done])

        EJ = CH // C
        NJ = E // EJ
        FT = NB * NT
        HB = sb("f_halves", [P, NB, 2, KT, N], F16)
        TB = sb("f_tokens", [P, NB, KT, N], F32)
        cb = sb("f_coef", [P, NB * NT * E], F32)
        acc = sb("f_acc", [P, 2, C], F32)
        fsem = [sem(n) for n in ("f_in0", "f_in1", "f_full", "f_coef", "f_acc", "f_turned", "f_added", "f_out")]
        f_in0, f_in1, f_full, f_cf, f_acc, f_t, f_x, f_out = fsem
        f_in = (f_in0, f_in1)
        NPB = 6

        def load_tokens(sp, s, b, signal):
            sp.dma_start(HB[:, s], batch(h_dram, b).rearrange("a p s k n -> (a p) s k n")).then_inc(signal, 16)
            sp.dma_start(TB[:, s], batch(t_dram, b).rearrange("a p k n -> (a p) k n")).then_inc(signal, 16)

        with nc.Block() as block:
            @block.sync
            def _(sp):
                load_tokens(sp, 0, 0, f_in0)
                sp.wait_ge(f_in0, 32)
        reset(fsem)

        with nc.Fori(0, B // NB) as i_:
            with nc.Block() as block:

                @block.sync
                def _(sp):
                    b0 = i_ * NB
                    load_tokens(sp, 1, b0 + 1, f_in1)
                    for s in range(NB):
                        sp.wait_ge(f_x, (s + 1) * NT)
                        sp.dma_start(batch(out, b0 + s).rearrange("a (k p) n -> (a p) k n", p=P), TB[:, s]).then_inc(f_out, 16)
                        if s == 0:
                            sp.wait_ge(f_out, 16)
                            load_tokens(sp, 0, (b0 + NB) % B, f_in0)
                    sp.wait_ge(f_in0, 32)
                    sp.wait_ge(f_out, 16 * NB)

                @block.tensor
                def _(pe):
                    def back(t):
                        pe.wait_ge(f_acc, (t + 1) * E)
                        if t >= 2:
                            pe.wait_ge(f_x, t - 1)
                        for k in range(KT):
                            last = nc.tensor.transpose(PS[:, NPB + t % 2, k * P:(k + 1) * P], acc[:, t % 2, k * P:(k + 1) * P], idf[:])
                        last.then_inc(f_t, 1)

                    for t in range(FT):
                        s_, tt = divmod(t, NT)
                        if t == NT:
                            pe.wait_ge(f_in1, 32)
                        for q in range(NJ):
                            n = t * NJ + q
                            if n >= NPB:
                                pe.wait_ge(f_acc, (n - NPB + 1) * EJ)
                            i = 0
                            for k in range(KT):
                                for s, w in ((0, 0), (0, 1), (1, 0)):
                                    last = nc.tensor.matmul(PS[:, n % NPB, :], HB[:, s_, s, k, tt * P:(tt + 1) * P],
                                                            ex_p[:, w, k, q * CH:(q + 1) * CH],
                                                            start=(i == 0), stop=(i == 3 * KT - 1))
                                    i += 1
                            last.then_inc(f_full, 1)
                            if q == 1 and t >= 1:
                                back(t - 1)
                    back(FT - 1)

                @block.vector
                def _(dve):
                    def add_back(t):
                        dve.wait_ge(f_t, t + 1)
                        s_, tt = divmod(t, NT)
                        if t == NT:
                            dve.wait_ge(f_in1, 32)
                        x_ = TB[:, s_, :, tt * P:(tt + 1) * P]
                        nc.vector.tensor_tensor(x_, x_, PS[:, NPB + t % 2, 0:C].rearrange("p (k n) -> p k n", k=KT),
                                                ALU.add).then_inc(f_x, 1)

                    nc.vector.tensor_scalar(cb[:], coef[:, bass.ds(i_ * (NB * NT * E), NB * NT * E)], 1.0 / WS, None,
                                            ALU.mult).then_inc(f_cf, 1)
                    dve.wait_ge(f_cf, 1)
                    for t in range(FT):
                        for e in range(E):
                            n = (t * E + e) // EJ
                            if e % EJ == 0:
                                dve.wait_ge(f_full, n + 1)
                            if e == 0 and t >= 2:
                                dve.wait_ge(f_t, t - 1)
                            ps = PS[:, n % NPB, (e % EJ) * C:(e % EJ + 1) * C]
                            c_e = cb[:, t * E + e:t * E + e + 1]
                            if e == 0:
                                ins = nc.vector.tensor_scalar(acc[:, t % 2, :], ps, c_e, None, ALU.mult)
                            else:
                                dve.wait_ge(f_acc, t * E + e)
                                ins = nc.vector.scalar_tensor_tensor(out=acc[:, t % 2, :], in0=ps, scalar=c_e,
                                                                     in1=acc[:, t % 2, :], op0=ALU.mult, op1=ALU.add)
                            ins.then_inc(f_acc, 1)
                            if e == 3 and t >= 1:
                                add_back(t - 1)
                    add_back(FT - 1)

            reset(fsem)


def kernel(**inputs):
    import numpy as np
    import concourse.bacc as _bacc
    from concourse import mybir as _mybir
    from concourse.bass_utils import run_bass_kernel_spmd as _run

    a = {k: np.asarray(v) for k, v in inputs.items()}
    B, C, HH, WW = a["x"].shape
    N, H = HH * WW, 8
    D = C // H
    con = np.ascontiguousarray
    wqkv = con(a["L0_conv_w_qkv"].T)
    wout = con(a["L0_conv_w_out"].T)
    w1 = a["L1_attn_W"].reshape(C, H, 3, D)
    b1 = a["L1_attn_b"].reshape(H, 3, D)
    swap = np.concatenate([np.arange(D // 2, D), np.arange(D // 2)])
    w1q = con(np.concatenate([w1[:, :, 0].reshape(C, C), w1[:, :, 0][:, :, swap].reshape(C, C),
                              w1[:, :, 1].reshape(C, C), w1[:, :, 2].reshape(C, C)], axis=1))
    cols = [b1[:, 0].reshape(-1, 128), b1[:, 0][:, swap].reshape(-1, 128), b1[:, 1].reshape(-1, 128)]
    b1cols = con(np.concatenate(cols, axis=0).T)
    b1v = con(b1[:, 2].reshape(-1))
    r = np.arange(-(WW - 1), WW, dtype=np.float32)
    lr = (-np.sign(r) * np.log(np.abs(r) + np.float32(1.0))).astype(np.float32)
    relt = con(np.stack([np.repeat(lr, len(r)), np.tile(lr, len(r))]))
    div = np.exp(-np.arange(0, D, 2, dtype=np.float32) * np.float32(np.log(10000.0) / D)).astype(np.float64)
    ang = div[:, None] * np.arange(N)[None, :]
    s, c = np.sin(ang), np.cos(ang)
    rot = np.stack([np.tile(np.concatenate([s, s]), (128 // D, 1)), np.tile(np.concatenate([c, -c]), (128 // D, 1))],
                   axis=1).astype(np.float32)
    etab = np.concatenate([c, s]).astype(np.float32)
    data = {
        "x": con(a["x"].reshape(B, C, N)),
        "gamma": con(a["L0_conv_gamma"].reshape(-1, 128).T),
        "wqkv": wqkv, "wout": wout, "w1q": w1q, "b1cols": b1cols, "b1v": b1v,
        "gatew": con(a["L1_ffn_gate_weight"][0]), "experts": con(a["L1_ffn_experts"]),
        "relt": relt,
        "cw0": con(a["L0_conv_cpb_w0"].T), "cb0": con(a["L0_conv_cpb_b0"][:, None]),
        "cw1": con(a["L0_conv_cpb_w1"].T), "cb1": con(a["L0_conv_cpb_b1"][:, None]),
        "cw2": con(a["L0_conv_cpb_w2"].T), "cb2": con(a["L0_conv_cpb_b2"][:, None]),
        "ident": np.eye(128, dtype=np.float32), "rot": con(rot), "etab": con(etab),
    }
    nc = _bacc.Bacc("TRN2", target_bir_lowering=False, num_devices=1)
    args = {k: nc.dram_tensor(f"in_{k}", list(v.shape), _mybir.dt.from_np(v.dtype), kind="ExternalInput").ap()
            for k, v in data.items()}
    out = nc.dram_tensor("out_0", [B, C, N], _mybir.dt.float32, kind="ExternalOutput").ap()
    build(nc, **args, out=out)
    res = _run(nc, [{f"in_{k}": v for k, v in data.items()}], core_ids=[0])
    return res.results[0]["out_0"].reshape(B, C, HH, WW)
```

```python
import concourse.bass as bass
from concourse import mybir
from contextlib import ExitStack


def build(nc, x, gamma, wqkv, wout, w1q, b1cols, b1v, gatew, experts, relt, cw0, cb0, cw1, cb1, cw2, cb2,
          ident, rot, etab, out):
    F32, F16 = mybir.dt.float32, mybir.dt.float16
    ALU = mybir.AluOpType
    ACT = mybir.ActivationFunctionType
    AX = mybir.AxisListType

    B, C, N = x.shape
    P = 128
    KT = C // P
    NT = N // P
    H, D = 8, C // 8
    G = H * D // P
    HG = H // G
    W = 32
    SIDE = 2 * W - 1
    ROWS = P // W
    ZU = 2 * W - ROWS
    E = gatew.shape[1]
    M = N // E
    WS = 64.0
    QS = float(D) ** -0.5
    CH = 512
    NC = N // CH
    EPS = 1e-5
    GATE_EPS = 1e-6
    SINKHORN = 8
    RC = 7 * SIDE
    NR = SIDE * SIDE // RC
    UN = NT * G
    ST_N = UN * HG
    PRING = 9
    NB = 4
    KTU = NT
    TLAG = HG + 1

    tdram = nc.dram_tensor("bias_table", [H, SIDE * SIDE], F32).ap()
    wdram = nc.dram_tensor("bias_windows", [W, H, SIDE * W], F32).ap()
    edram = nc.dram_tensor("rel_embedding_halves", [2 * D, N], F16).ap()
    qk_dram = [nc.dram_tensor(f"query_key_halves_{i}", [B, G, (4, 6)[i], P, N], F16).ap() for i in range(2)]
    v_dram = [nc.dram_tensor(f"values_{i}", [B, P, NT, C], F32).ap() for i in range(2)]
    o_dram = nc.dram_tensor("attended_halves", [B, P, 2, KT, N], F16).ap()
    x1_dram = nc.dram_tensor("tokens_after_first", [B, P, KT, N], F32).ap()
    t_dram = nc.dram_tensor("tokens_after_attention", [B, P, KT, N], F32).ap()
    h_dram = nc.dram_tensor("normed_halves", [B, P, 2, KT, N], F16).ap()

    ctx = ExitStack()
    with ctx:
        def sb(name, shape, dt):
            return ctx.enter_context(nc.sbuf_tensor(name, shape, dt))

        def sem(name):
            return ctx.enter_context(nc.semaphore(name))

        wqkv_p = sb("wqkv_p", [P, 2, KT, 3 * C], F16)
        wout_p = sb("wout_p", [P, 2, KT, C], F16)
        w1_p = sb("w1_p", [P, 2, KT, 4 * C], F16)
        gate_p = sb("gate_p", [P, 2, KT, E], F16)
        gates = sb("gates", [P, B * NT * E], F32)
        idf = sb("idf", [P, P], F32)
        ones = sb("ones", [P, P], F32)
        idh = sb("idh", [P, P], F16)
        ones_h = sb("ones_h", [P, P], F16)
        bvb = sb("bvb", [P, C], F32)
        bcol = sb("bcol", [P, 6], F32)
        eps = sb("eps", [P, 1], F32)
        bias = sb("bias", [P, H, ZU * W], F32)
        zf = bias[:, :, :].rearrange("p h z -> p (h z)")

        PS = ctx.enter_context(nc.psum_tensor("PS", [P, 8, CH], F32))

        def reset(sems):
            nums = sorted(s.num for s in sems)
            first = [n for n in nums if n - 1 not in nums]
            for a, b in zip(first, [n for n in nums if n + 1 not in nums]):
                nc.sync.sem_clear(range(a, b + 1))
            nc.all_engine_barrier()

        with ExitStack() as es:
            def ssem(name):
                return es.enter_context(nc.semaphore(name))

            w_sum = KT * (3 * C + C + 4 * C + E)
            flat = es.enter_context(nc.sbuf_tensor("set_scratch", [P, 6 * N], F32))
            w_st = es.enter_context(nc.sbuf_tensor("set_weights", [P, w_sum + 256], F32))
            rel = zf[0:2, 0:SIDE * SIDE]
            h0 = zf[0:64, SIDE * SIDE:2 * SIDE * SIDE]
            h1 = zf[0:64, 2 * SIDE * SIDE:3 * SIDE * SIDE]
            tab = flat[0:H, 0:SIDE * SIDE]
            e_f = flat[0:D, 4 * N:5 * N]
            e_p = flat[0:D, 5 * N:6 * N].bitcast(F16).rearrange("p (s n) -> p s n", s=2)

            WL = []
            off = 0
            for src, dst, cols in ((wqkv, wqkv_p, 3 * C), (wout, wout_p, C), (w1q, w1_p, 4 * C), (gatew, gate_p, E)):
                WL.append((src, dst, w_st[:, off:off + KT * cols].rearrange("p (k n) -> p k n", k=KT)))
                off += KT * cols
            small = w_st[:, off:off + 256]
            c_w0, c_w1, c_w2 = small[0:2, 0:64], small[0:64, 64:128], small[0:64, 128:128 + H]
            c_b0, c_b1, c_b2 = small[0:64, 140:141], small[0:64, 141:142], small[0:H, 142:143]
            gam = small[:, 144:144 + KT]

            net_in, w_in, g_in, cst_in, e_in = (ssem(n) for n in ("net_in", "w_in", "g_in", "cst_in", "e_in"))
            net_mm, net_act, net_dve = ssem("net_mm"), ssem("net_act"), ssem("net_dve")
            w_scaled, w_high, w_low = ssem("w_scaled"), ssem("w_high"), ssem("w_low")
            tab_out, e_out, e_high, e_low, win_out = (ssem(n) for n in ("tab_out", "e_out", "e_high", "e_low", "win_out"))
            BP = 4
            blk = ExitStack()
            block = blk.enter_context(nc.Block())
            NETL = 3 * NR

            @block.sync
            def _(sp):
                for dst, src in ((rel, relt), (c_w0, cw0), (c_w1, cw1), (c_w2, cw2), (c_b0, cb0), (c_b1, cb1),
                                 (c_b2, cb2)):
                    sp.dma_start(dst, src).then_inc(net_in, 16)
                sp.dma_start(gam, gamma).then_inc(g_in, 16)
                for src, _, st in WL:
                    sp.dma_start(st, src.rearrange("(k p) n -> p k n", p=P)).then_inc(w_in, 16)
                sp.dma_start(e_f, etab).then_inc(e_in, 16)
                sp.dma_start(idf[:], ident).then_inc(cst_in, 16)
                sp.dma_start(bcol[:], b1cols).then_inc(cst_in, 16)
                sp.dma_start(bvb[:], b1v.partition_broadcast(P)).then_inc(cst_in, 16)
                sp.wait_ge(e_low, 1)
                for s in range(2):
                    sp.dma_start(edram[s * D:(s + 1) * D, :], e_p[:, s, :]).then_inc(e_out, 16)
                sp.wait_ge(net_act, NETL)
                sp.dma_start(tdram, tab).then_inc(tab_out, 16)
                sp.wait_ge(tab_out, 16)
                HR = H * SIDE // BP
                for n in range(BP):
                    sp.dma_start(bass.AP(wdram.tensor, n * HR * W, [[W, HR], [H * SIDE * W, W], [1, W]]),
                                 bass.AP(tdram.tensor, n * HR * SIDE + W - 1, [[SIDE, HR], [-1, W], [1, W]])
                                 ).then_inc(win_out, 16)
                sp.wait_ge(win_out, 16 * BP)
                sp.wait_ge(e_out, 32)
                sp.wait_ge(cst_in, 48)

            @block.tensor
            def _(pe):
                pe.wait_ge(net_in, 7 * 16)
                for layer, (w_, src, rows) in enumerate(((c_w0, rel, 64), (c_w1, h0, 64), (c_w2, h1, H))):
                    for c in range(NR):
                        n = layer * NR + c
                        if n >= 4:
                            pe.wait_ge(net_act, n - 3)
                        if layer:
                            pe.wait_ge(net_dve, n - NR + 1)
                        nc.tensor.matmul(PS[0:rows, n % 4, 0:RC], w_, src[:, c * RC:(c + 1) * RC],
                                         start=True, stop=True).then_inc(net_mm, 1)

            @block.scalar
            def _(act):
                for layer, (dst, b_, rows) in enumerate(((h0, c_b0, 64), (h1, c_b1, 64), (tab, c_b2, H))):
                    for c in range(NR):
                        n = layer * NR + c
                        act.wait_ge(net_mm, n + 1)
                        nc.scalar.activation(dst[:, c * RC:(c + 1) * RC], PS[0:rows, n % 4, 0:RC], ACT.Identity,
                                             bias=b_).then_inc(net_act, 1)
                act.wait_ge(e_in, 16)
                nc.scalar.copy(e_p[:, 0, :], e_f).then_inc(e_high, 1)
                act.wait_ge(cst_in, 48)
                nc.scalar.copy(idh[:], idf[:])
                for n, (_, dst, st) in enumerate(WL):
                    act.wait_ge(w_scaled, KT * (n + 1))
                    nc.scalar.copy(dst[:, 0, :, :], st).then_inc(w_high, 1)

            @block.gpsimd
            def _(pool):
                nc.gpsimd.memset(ones[:], 1.0 / C)
                nc.gpsimd.memset(ones_h[:], 1.0 / C)
                nc.gpsimd.memset(eps[:], EPS)

            @block.vector
            def _(dve):
                for layer, dst in enumerate((h0, h1)):
                    for c in range(NR):
                        n = layer * NR + c
                        dve.wait_ge(net_act, n + 1)
                        v = dst[:, c * RC:(c + 1) * RC]
                        nc.vector.scalar_tensor_tensor(out=v, in0=v, scalar=0.1, in1=v, op0=ALU.mult,
                                                       op1=ALU.max).then_inc(net_dve, 1)
                dve.wait_ge(g_in, 16)
                dve.wait_ge(w_in, 16 * len(WL))
                for n, (_, dst, st) in enumerate(WL):
                    for k in range(KT):
                        if n == 0:
                            nc.vector.tensor_scalar(st[:, k, :], st[:, k, :], gam[:, k:k + 1], WS, ALU.mult,
                                                    ALU.mult).then_inc(w_scaled, 1)
                        else:
                            nc.vector.tensor_scalar(st[:, k, :], st[:, k, :], WS, None, ALU.mult).then_inc(w_scaled, 1)
                for n, (_, dst, st) in enumerate(WL):
                    dve.wait_ge(w_high, n + 1)
                    nc.vector.tensor_tensor(dst[:, 1, :, :], st, dst[:, 0, :, :], ALU.subtract)
                dve.wait_ge(e_high, 1)
                nc.vector.tensor_tensor(e_p[:, 1, :], e_f, e_p[:, 0, :], ALU.subtract).then_inc(e_low, 1)
                dve.wait_ge(cst_in, 48)
                nc.vector.tensor_scalar(bcol[:, 0:4], bcol[:, 0:4], -QS, None, ALU.mult)

            blk.close()
            reset([net_in, w_in, g_in, cst_in, e_in, net_mm, net_act, net_dve, w_scaled, w_high, w_low, tab_out, e_out,
                   e_high, e_low, win_out])

        def batch(dram, b):
            return dram[bass.ds(b, 1)]

        TB_ = 4
        NCH = TB_ * NC
        TT = CH // P
        HS = H * TB_ // B

        def token_phase(kind):
            with ExitStack() as es:
                def ssem(name):
                    return es.enter_context(nc.semaphore(f"{name}_{kind}"))

                def tile(name, shape, dt):
                    return es.enter_context(nc.sbuf_tensor(f"{name}_{kind}", shape, dt))

                NQ = (2 * G, 3 * G, 0)[kind]
                NV = (2, 2, 0)[kind]
                NP = (0, KT, 0)[kind]
                STG = (4, 6, 0)[kind]
                wp = (wqkv_p, w1_p, gate_p)[kind]
                XR = 4
                xin = tile("xin", [P, XR, KT, CH], F32)
                xc = tile("xc", [P, 3, KT, CH], F32)
                sq = tile("sq", [P, KT, CH], F32)
                xs = tile("xs", [P, 2, 2, KT, CH], F16)
                sqs = tile("sqs", [P, 2, 2, KT, CH], F16)
                rstd = tile("rstd", [P, 2, TT], F32)
                rstd_h = tile("rstd_h", [P, 2, 2, TT], F16)
                xh = tile("xh", [P, 3, KT, CH], F16)
                xl = tile("xl", [P, 3, KT, CH], F16)
                if kind < 2:
                    stg = tile("stg", [P, 2, G, STG, CH], F16)
                    vst = tile("vst", [P, 2, TT, C], F32)
                if kind == 1:
                    oin = tile("oin", [P, 2, 2, KT, CH], F16)
                    rots = tile("rots", [P, 2, N], F32)
                    qf = tile("qf", [P, 2, CH], F32)
                    qsf = tile("qsf", [P, 2, CH], F32)
                    rf = tile("rf", [P, 2, CH], F32)
                    kf = tile("kf", [P, 2, CH], F32)

                sems = [ssem(n) for n in ("full", "res", "centred", "x_high", "x_low", "sq_ok", "sq_high", "sq_low", "std", "rstd_ok", "rstd_high", "rstd_low",
                                          "scaled", "high", "low", "q_high", "kf_ok", "qf_ok", "qs_ok", "turned",
                                          "added", "k_high", "q_low", "vals", "gated", "rot_in", "bias_in")]
                (full, res, centred, x_high, x_low, sq_ok, sq_high, sq_low, std, rstd_ok, rstd_high, rstd_low, scaled, high, low, q_high, kf_ok,
                 qf_ok, qs_ok, turned, added, k_high, q_low, vals, gated, rot_in, bias_in) = sems
                SR = 3 if kind == 2 else 2
                loaded, o_loaded, stored, v_stored, x_stored = (
                    [ssem(f"{n}{i}") for i in range(XR)] for n in ("loaded", "o_loaded", "stored", "v_stored", "x_stored"))
                sems += loaded + o_loaded + stored + v_stored + x_stored

                AHEAD = XR if kind != 1 else 2

                def wait_loaded(engine, u):
                    n = u // XR + (u % XR >= AHEAD)
                    if n:
                        engine.wait_ge(loaded[u % XR], 16 * n)

                def wait_tokens(engine, u):
                    if kind == 1:
                        engine.wait_ge(res, KT * (u + 1))
                    else:
                        wait_loaded(engine, u)

                def is_stored(u):
                    return stored[u % SR], 32 * (u // SR + 1)

                order = []
                for u in range(-3, NCH):
                    n_, w_ = u + 3, u + 2
                    a = [("proj", n_, m) for m in range(NP)] if n_ < NCH else []
                    first = [("qk", u, m) for m in range(NQ // 2)] if u >= 0 else []
                    mean = [("mean", n_, 0)] if n_ < NCH else []
                    second = [("qk", u, m) for m in range(NQ // 2, NQ)] if u >= 0 else []
                    var = [("var", w_, 0)] if 0 <= w_ < NCH else []
                    rsd = [("rsd", w_, 0)] if 0 <= w_ < NCH else []
                    v = [("v", u, m) for m in range(NV)] if u >= 0 else []
                    g_ = [("gate", u, 0)] if kind == 2 and u >= 0 else []
                    order += (var + first + mean + rsd + second + v, a + first + var + second + rsd + mean + v,
                              var + mean + g_ + rsd)[kind]
                at = {n: i for i, n in enumerate(order)}
                if kind == 1:
                    halved_first, halved_at = [], {("proj", u, KT - 1): u for u in range(NCH)}
                else:
                    halved_first, halved_at = [0, 1], {("var", u, 0): u + 2 for u in range(NCH - 2)}

                def read_out(name):
                    what, u, m = name
                    if what == "qk":
                        if kind == 0:
                            return q_low, u * NQ + m + 1
                        return (qf_ok, qs_ok, kf_ok)[m % 3], u * G + m // 3 + 1
                    return {"proj": (res, KT * u + m + 1), "mean": (centred, KT * (u + 1)), "var": (std, u + 1),
                            "rsd": (scaled, KT * (u + 1)), "v": (vals, NV * u + m + 1), "gate": (gated, u + 1)}[what]

                def bank(name):
                    return PS[:, at[name] % 8, :]

                def last_use(u):
                    if kind == 2:
                        return is_stored(u)
                    return full, at[("v", u, NV - 1)] + 1

                def load_chunk(sp, u, b):
                    tok = slice((u % NC) * CH, (u % NC + 1) * CH)
                    if kind == 1:
                        sp.dma_start(oin[:, u % 2], batch(o_dram, b)[:, :, :, :, tok].rearrange(
                            "a p s k n -> (a p) s k n")).then_inc(o_loaded[u % 2], 16)
                    if kind < 2:
                        src = batch(x, b)[:, :, tok].rearrange("a (k p) n -> (a p) k n", p=P)
                    else:
                        src = batch(t_dram, b)[:, :, :, tok].rearrange("a p k n -> (a p) k n")
                    sp.dma_start(xin[:, u % XR], src).then_inc(loaded[u % XR], 16)

                with nc.Block() as block:
                    @block.sync
                    def _(sp):
                        if kind == 1:
                            sp.dma_start(rots[:, :, :], rot).then_inc(rot_in, 16)
                        for u in range(AHEAD):
                            load_chunk(sp, u, u // NC)
                        for u in range(AHEAD):
                            sp.wait_ge(loaded[u], 16)
                            if kind == 1:
                                sp.wait_ge(o_loaded[u], 16)
                        if kind == 1:
                            sp.wait_ge(rot_in, 16)
                reset(sems)

                with nc.Fori(0, B // TB_) as i:
                    with nc.Block() as block:

                        def where(u):
                            b = i * TB_ + u // NC
                            return b if u < NCH else b % B, slice((u % NC) * CH, (u % NC + 1) * CH)

                        @block.sync
                        def _(sp):
                            def load(u):
                                if u >= XR:
                                    sp.wait_ge(centred, KT * (u - XR + 1))
                                if kind == 1:
                                    if u >= XR:
                                        sp.wait_ge(x_stored[u % XR], 16 * (u // XR))
                                    sp.wait_ge(full, at[("proj", u - 2, KT - 1)] + 1)
                                load_chunk(sp, u, where(u)[0])

                            def store(u):
                                b, tok = where(u)
                                if kind == 2:
                                    sp.wait_ge(high, KT * (u + 1))
                                    sp.wait_ge(low, KT * (u + 1))
                                    for s, t_ in enumerate((xh, xl)):
                                        sp.dma_start(batch(h_dram, b)[:, :, s, :, tok].rearrange("a p k n -> (a p) k n"),
                                                     t_[:, u % 3]).then_inc(stored[u % SR], 16)
                                    return
                                for g in range(G):
                                    sp.wait_ge(q_low, (u * G + g + 1) * (STG // 2))
                                    sp.dma_start(batch(qk_dram[kind], b)[:, g, :, :, tok].rearrange("a s p n -> (a p) s n"),
                                                 stg[:, u % 2, g]).then_inc(stored[u % SR], 16)
                                sp.wait_ge(vals, NV * (u + 1))
                                sp.dma_start(batch(v_dram[kind], b)[:, :, (u % NC) * TT:(u % NC + 1) * TT].rearrange(
                                    "a p t c -> (a p) t c"), vst[:, u % 2]).then_inc(v_stored[u % 2], 16)

                            for u in range(-3, NCH):
                                if kind == 1 and u + 3 < NCH:
                                    b, tok = where(u + 3)
                                    sp.wait_ge(res, KT * (u + 4))
                                    sp.dma_start(batch(x1_dram, b)[:, :, :, tok].rearrange("a p k n -> (a p) k n"),
                                                 xin[:, (u + 3) % XR]).then_inc(x_stored[(u + 3) % XR], 16)
                                if u + 3 < NCH:
                                    load(u + 3 + AHEAD)
                                if kind == 0 and 0 <= u < ROWS:
                                    sp.dma_start(bias[u * W:(u + 1) * W, bass.ds(i * HS, HS), :],
                                                 wdram[:, bass.ds(i * HS, HS), (ROWS - 1 - u) * W:(ROWS - 1 - u + ZU) * W]
                                                 ).then_inc(bias_in, 16)
                                if u >= 0:
                                    store(u)
                            if kind == 0:
                                sp.wait_ge(bias_in, 16 * ROWS)
                            for u in range(AHEAD):
                                sp.wait_ge(loaded[u], 16 * (NCH // XR))
                                if kind == 1:
                                    sp.wait_ge(o_loaded[u], 16 * (NCH // 2))
                            for u in range(NCH - XR, NCH):
                                if u >= NCH - SR:
                                    sp.wait_ge(*is_stored(u))
                                if kind < 2 and u >= NCH - 2:
                                    sp.wait_ge(v_stored[u % 2], 16 * (u // 2 + 1))
                                if kind == 1:
                                    sp.wait_ge(x_stored[u % XR], 16 * (u // XR + 1))

                        @block.tensor
                        def _(pe):
                            def product(u, out, wts, col, halves):
                                n = 0
                                for k in range(KT):
                                    for part, s in ((0, 0), (0, 1), (1, 0)):
                                        last = nc.tensor.matmul(out, wts[:, part, k, col:col + P], halves(s, k),
                                                                start=(n == 0), stop=(n == 3 * KT - 1))
                                        n += 1
                                return last

                            def tokens_first(u, out, tok, wts, col, cols):
                                n = 0
                                for k in range(KT):
                                    for src, part in ((xh, 0), (xh, 1), (xl, 0)):
                                        last = nc.tensor.matmul(out, src[:, u % 3, k, tok], wts[:, part, k, col:col + cols],
                                                                start=(n == 0), stop=(n == 3 * KT - 1))
                                        n += 1
                                return last

                            normed = set()
                            for name in order:
                                what, u, m = name
                                n = at[name]
                                if n >= 8:
                                    reader, count = read_out(order[n - 8])
                                    pe.wait_ge(reader, count)
                                if what in ("qk", "v", "gate") and u not in normed:
                                    normed.add(u)
                                    pe.wait_ge(high, KT * (u + 1))
                                    pe.wait_ge(low, KT * (u + 1))
                                ps = bank(name)
                                if what == "proj":
                                    if u >= AHEAD:
                                        pe.wait_ge(o_loaded[u % 2], 16 * (u // 2))
                                    last = product(u, ps, wout_p, m * P, lambda s, k: oin[:, u % 2, s, k, :])
                                elif what == "mean":
                                    pe.wait_ge(x_low, KT * (u + 1))
                                    for h in range(2):
                                        for k in range(KT):
                                            last = nc.tensor.matmul(ps, ones_h[:], xs[:, u % 2, h, k, :],
                                                                    start=(h + k == 0), stop=(h + k == KT))
                                elif what == "var":
                                    pe.wait_ge(sq_low, KT * (u + 1))
                                    for t in range(TT):
                                        for h in range(2):
                                            for k in range(KT):
                                                last = nc.tensor.matmul(ps[:, t:t + 1], sqs[:, u % 2, h, k, t * P:(t + 1) * P],
                                                                        ones_h[:, 0:1], start=(h + k == 0), stop=(h + k == KT))
                                elif what == "rsd":
                                    pe.wait_ge(rstd_low, u + 1)
                                    for t in range(TT):
                                        for h in range(2):
                                            last = nc.tensor.matmul(ps[:, t * P:(t + 1) * P],
                                                                    rstd_h[:, u % 2, h, t:t + 1].broadcast_to([P, P]), idh[:],
                                                                    start=(h == 0), stop=(h == 1))
                                elif what == "qk":
                                    col = (m % 2) * C + (m // 2) * P if kind == 0 else (m % 3) * C + (m // 3) * P
                                    last = product(u, ps, wp, col, lambda s, k: (xh, xl)[s][:, u % 3, k, :])
                                elif what == "v":
                                    for t in range(2):
                                        last = tokens_first(u, ps[:, t * C:(t + 1) * C],
                                                            slice((2 * m + t) * P, (2 * m + t + 1) * P), wp,
                                                            (2 + kind) * C, C)
                                else:
                                    for t in range(TT):
                                        last = tokens_first(u, ps[:, t * E:(t + 1) * E], slice(t * P, (t + 1) * P),
                                                            gate_p, 0, E)
                                last.then_inc(full, 1)

                        @block.scalar
                        def _(act):
                            def stage_free(u):
                                if u >= 2:
                                    act.wait_ge(*is_stored(u - 2))

                            def high_tokens(u):
                                wait_tokens(act, u)
                                if u >= 2:
                                    act.wait_ge(full, at[("mean", u - 2, 0)] + 1)
                                for k in range(KT):
                                    nc.scalar.copy(xs[:, u % 2, 0, k, :], xin[:, u % XR, k, :]).then_inc(x_high, 1)

                            for u in halved_first:
                                high_tokens(u)
                            for name in order:
                                what, u, m = name
                                n = at[name]
                                if what == "mean":
                                    for k in range(KT):
                                        act.wait_ge(centred, KT * u + k + 1)
                                        if u >= 1:
                                            act.wait_ge(sq_low, KT * (u - 1) + k + 1)
                                        nc.scalar.activation(sq[:, k, :], xc[:, u % 3, k, :], ACT.Square).then_inc(sq_ok, 1)
                                        if u >= 2:
                                            act.wait_ge(full, at[("var", u - 2, 0)] + 1)
                                        nc.scalar.activation(sqs[:, u % 2, 0, k, :], xc[:, u % 3, k, :],
                                                             ACT.Square).then_inc(sq_high, 1)
                                elif what == "var":
                                    act.wait_ge(full, n + 1)
                                    if u >= 2:
                                        act.wait_ge(rstd_low, u - 1)
                                    nc.scalar.activation(rstd[:, u % 2, :], bank(name)[:, 0:TT], ACT.Sqrt,
                                                         bias=eps[:]).then_inc(std, 1)
                                elif what == "qk" and kind == 0:
                                    act.wait_ge(full, n + 1)
                                    stage_free(u)
                                    nc.scalar.activation(stg[:, u % 2, m // 2, 2 * (m % 2), :], bank(name), ACT.Copy,
                                                         scale=(QS if m % 2 == 0 else 1.0) / WS).then_inc(q_high, 1)
                                elif what == "qk":
                                    g, w = divmod(m, 3)
                                    s = u * G + g
                                    if m == 0:
                                        stage_free(u)
                                    act.wait_ge(full, n + 1)
                                    if w == 0:
                                        if s >= 2:
                                            act.wait_ge(q_low, 3 * (s - 2) + 1)
                                            act.wait_ge(turned, 2 * (s - 2) + 1)
                                        nc.scalar.activation(qf[:, s % 2, :], bank(name), ACT.Identity, scale=-QS / WS,
                                                             bias=bcol[:, g:g + 1]).then_inc(qf_ok, 1)
                                        act.wait_ge(qf_ok, s + 1)
                                        nc.scalar.copy(stg[:, u % 2, g, 0, :], qf[:, s % 2, :]).then_inc(q_high, 1)
                                    elif w == 1:
                                        if s >= 2:
                                            act.wait_ge(q_low, 3 * (s - 2) + 2)
                                        nc.scalar.activation(qsf[:, s % 2, :], bank(name), ACT.Identity, scale=-QS / WS,
                                                             bias=bcol[:, 2 + g:3 + g]).then_inc(qs_ok, 1)
                                    else:
                                        if s >= 2:
                                            act.wait_ge(q_low, 3 * (s - 2) + 3)
                                        nc.scalar.activation(kf[:, s % 2, :], bank(name), ACT.Identity, scale=1.0 / WS,
                                                             bias=bcol[:, 4 + g:5 + g]).then_inc(kf_ok, 1)
                                        act.wait_ge(kf_ok, s + 1)
                                        nc.scalar.copy(stg[:, u % 2, g, 4, :], kf[:, s % 2, :]).then_inc(k_high, 1)
                                        act.wait_ge(added, s + 1)
                                        nc.scalar.copy(stg[:, u % 2, g, 2, :], qsf[:, s % 2, :]).then_inc(q_high, 1)
                                elif what == "v" and kind == 0:
                                    act.wait_ge(full, n + 1)
                                    if u >= 2:
                                        act.wait_ge(v_stored[u % 2], 16 * (u // 2))
                                    nc.scalar.activation(vst[:, u % 2, 2 * m:2 * m + 2, :].rearrange("p t c -> p (t c)"),
                                                         bank(name), ACT.Copy, scale=1.0 / WS).then_inc(vals, 1)
                                if name in halved_at:
                                    high_tokens(halved_at[name])
                                if what == "rsd":
                                    for k in range(KT):
                                        act.wait_ge(scaled, KT * u + k + 1)
                                        if u >= 3 and k == 0:
                                            act.wait_ge(*last_use(u - 3))
                                        nc.scalar.copy(xh[:, u % 3, k, :], xc[:, u % 3, k, :]).then_inc(high, 1)

                        @block.gpsimd
                        def _(pool):
                            def low_tokens(u):
                                for k in range(KT):
                                    pool.wait_ge(x_high, KT * u + k + 1)
                                    nc.gpsimd.tensor_tensor(xs[:, u % 2, 1, k, :], xin[:, u % XR, k, :], xs[:, u % 2, 0, k, :],
                                                            ALU.subtract).then_inc(x_low, 1)

                            for u in halved_first:
                                low_tokens(u)
                            for name in order:
                                what, u, m = name
                                if what == "mean":
                                    for k in range(KT):
                                        pool.wait_ge(sq_ok, KT * u + k + 1)
                                        pool.wait_ge(sq_high, KT * u + k + 1)
                                        nc.gpsimd.tensor_tensor(sqs[:, u % 2, 1, k, :], sq[:, k, :], sqs[:, u % 2, 0, k, :],
                                                                ALU.subtract).then_inc(sq_low, 1)
                                elif what == "qk" and kind == 1 and m % 3 == 1:
                                    s = u * G + m // 3
                                    tok = slice((u % NC) * CH, (u % NC + 1) * CH)
                                    pool.wait_ge(qf_ok, s + 1)
                                    if s >= 2:
                                        pool.wait_ge(added, s - 1)
                                    nc.gpsimd.tensor_tensor(rf[:, s % 2, :], qf[:, s % 2, :], rots[:, 0, tok],
                                                            ALU.mult).then_inc(turned, 1)
                                    pool.wait_ge(qs_ok, s + 1)
                                    nc.gpsimd.tensor_tensor(qsf[:, s % 2, :], qsf[:, s % 2, :], rots[:, 1, tok],
                                                            ALU.mult).then_inc(turned, 1)
                                if name in halved_at:
                                    low_tokens(halved_at[name])

                        @block.vector
                        def _(dve):
                            for name in order:
                                what, u, m = name
                                n = at[name]
                                if what == "proj":
                                    dve.wait_ge(full, n + 1)
                                    wait_loaded(dve, u)
                                    nc.vector.scalar_tensor_tensor(out=xin[:, u % XR, m, :], in0=bank(name), scalar=1.0 / WS,
                                                                   in1=xin[:, u % XR, m, :], op0=ALU.mult,
                                                                   op1=ALU.add).then_inc(res, 1)
                                elif what == "mean":
                                    dve.wait_ge(full, n + 1)
                                    wait_tokens(dve, u)
                                    if u >= 3:
                                        dve.wait_ge(high, KT * (u - 2))
                                        dve.wait_ge(low, KT * (u - 2))
                                    for k in range(KT):
                                        nc.vector.tensor_tensor(xc[:, u % 3, k, :], xin[:, u % XR, k, :], bank(name),
                                                                ALU.subtract).then_inc(centred, 1)
                                elif what == "var":
                                    dve.wait_ge(std, u + 1)
                                    nc.vector.reciprocal(rstd[:, u % 2, :], rstd[:, u % 2, :]).then_inc(rstd_ok, 1)
                                    dve.wait_ge(rstd_ok, u + 1)
                                    if u >= 2:
                                        dve.wait_ge(full, at[("rsd", u - 2, 0)] + 1)
                                    nc.vector.tensor_copy(rstd_h[:, u % 2, 0, :], rstd[:, u % 2, :]).then_inc(rstd_high, 1)
                                    dve.wait_ge(rstd_high, u + 1)
                                    nc.vector.tensor_tensor(rstd_h[:, u % 2, 1, :], rstd[:, u % 2, :], rstd_h[:, u % 2, 0, :],
                                                            ALU.subtract).then_inc(rstd_low, 1)
                                elif what == "rsd":
                                    dve.wait_ge(full, n + 1)
                                    for k in range(KT):
                                        dve.wait_ge(sq_high, KT * u + k + 1)
                                        nc.vector.tensor_tensor(xc[:, u % 3, k, :], xc[:, u % 3, k, :], bank(name),
                                                                ALU.mult).then_inc(scaled, 1)
                                    if u >= 3:
                                        dve.wait_ge(*last_use(u - 3))
                                    for k in range(KT):
                                        dve.wait_ge(high, KT * u + k + 1)
                                        nc.vector.tensor_tensor(xl[:, u % 3, k, :], xc[:, u % 3, k, :], xh[:, u % 3, k, :],
                                                                ALU.subtract).then_inc(low, 1)
                                elif what == "qk" and kind == 0:
                                    dve.wait_ge(q_high, u * NQ + m + 1)
                                    s = stg[:, u % 2, m // 2]
                                    nc.vector.scalar_tensor_tensor(
                                        out=s[:, 2 * (m % 2) + 1, :], in0=bank(name), scalar=(QS if m % 2 == 0 else 1.0) / WS,
                                        in1=s[:, 2 * (m % 2), :], op0=ALU.mult, op1=ALU.subtract).then_inc(q_low, 1)
                                elif what == "qk":
                                    g, w = divmod(m, 3)
                                    s = u * G + g
                                    if w == 0:
                                        dve.wait_ge(q_high, 2 * s + 1)
                                        nc.vector.tensor_tensor(stg[:, u % 2, g, 1, :], qf[:, s % 2, :], stg[:, u % 2, g, 0, :],
                                                                ALU.subtract).then_inc(q_low, 1)
                                    elif w == 2:
                                        dve.wait_ge(turned, 2 * (s + 1))
                                        nc.vector.tensor_tensor(qsf[:, s % 2, :], rf[:, s % 2, :], qsf[:, s % 2, :],
                                                                ALU.add).then_inc(added, 1)
                                        dve.wait_ge(q_high, 2 * s + 2)
                                        nc.vector.tensor_tensor(stg[:, u % 2, g, 3, :], qsf[:, s % 2, :], stg[:, u % 2, g, 2, :],
                                                                ALU.subtract).then_inc(q_low, 1)
                                        dve.wait_ge(k_high, s + 1)
                                        nc.vector.tensor_tensor(stg[:, u % 2, g, 5, :], kf[:, s % 2, :], stg[:, u % 2, g, 4, :],
                                                                ALU.subtract).then_inc(q_low, 1)
                                elif what == "v" and kind == 1:
                                    dve.wait_ge(full, n + 1)
                                    if u >= 2:
                                        dve.wait_ge(v_stored[u % 2], 16 * (u // 2))
                                    nc.vector.scalar_tensor_tensor(
                                        out=vst[:, u % 2, 2 * m:2 * m + 2, :], in0=bank(name).rearrange("p (t c) -> p t c", t=2),
                                        scalar=1.0 / WS, in1=bvb[:].unsqueeze(1).broadcast_to([P, 2, C]), op0=ALU.mult,
                                        op1=ALU.add).then_inc(vals, 1)
                                elif what == "gate":
                                    dve.wait_ge(full, n + 1)
                                    b, tok = where(u)
                                    nc.vector.tensor_scalar(
                                        gates[:, bass.ds(b * (NT * E) + (u % NC) * TT * E, TT * E)], bank(name)[:, 0:TT * E],
                                        1.0 / WS, GATE_EPS, ALU.mult, ALU.max).then_inc(gated, 1)

                    reset(sems)

        def attention_queries_first():
            with ExitStack() as es:
                def ssem(name):
                    return es.enter_context(nc.semaphore(f"{name}_qf"))

                def tile(name, shape, dt):
                    return es.enter_context(nc.sbuf_tensor(f"{name}_qf", shape, dt))

                stacks = tile("stacks", [P, 2, 2, HG, N], F16)
                V = tile("V", [P, 2, NT, C], F32)
                ring = tile("ring", [P, PRING, N], F32)
                PTs = tile("PTs", [P, 3, CH], F32)
                nmax = tile("nmax", [P, NB * ST_N], F32)
                sums = tile("sums", [P, NB * ST_N], F32)
                rsum = tile("rsum", [P, 2, HG], F32)
                rsx = tile("rsx", [P, 2, P], F32)
                rbs = tile("rbs", [P, 2, P], F32)
                oF = tile("oF", [P, 2, P], F32)
                res_ = tile("res", [P, 2, 2, KT, N], F16)
                scores_ps = [PS[:, 2 * i:2 * i + 2, :].rearrange("p a n -> p (a n)") for i in range(2)]
                turned_ps = [PS[:, 4 + i, :] for i in range(2)]
                out_ps = [PS[:, 6 + i, :] for i in range(2)]

                NU = NB * UN
                NTL = NU * HG
                LK = NU * KTU
                NG = NB * G
                TG = NT * HG
                LOADS = 16 * 8

                sems = [ssem(n) for n in ("stk0", "stk1", "v_in0", "v_in1", "out_st0", "out_st1", "full", "nmx", "exps", "t_full", "ev_act", "ev_dve",
                                          "weighed", "rs1", "rs", "spread", "rb_copy", "of", "fin", "hi")]
                (stk0, stk1, v_in0, v_in1, out_st0, out_st1, full, nmx, exps, t_full, ev_act, ev_dve, weighed, rs1, rs, spread_, rb_copy, of,
                 fin, hi) = sems
                tev, v_in, stk, out_st = (ev_act, ev_dve), (v_in0, v_in1), (stk0, stk1), (out_st0, out_st1)

                def place(i):
                    u = i // HG
                    return u, i % HG, u // UN, (u // NT) % G, u % NT

                def load_group(sp, q, b, g):
                    src = batch(qk_dram[0], b)[:, g].rearrange("a s (j d) n -> d (a s) j n", d=D)
                    for r, st, s in [(r, 0, (0, 0, 1, 1)[r]) for r in range(4)] + [(r, 1, (2, 3, 2, 3)[r]) for r in range(4)]:
                        sp.dma_start(stacks[r * D:(r + 1) * D, q % 2, st], src[:, s]).then_inc(stk[q % 2], 16)

                def load_values(sp, n, b):
                    sp.dma_start(V[:, n % 2], batch(v_dram[0], b).rearrange("a p t c -> (a p) t c")).then_inc(v_in[n % 2], 16)

                with nc.Block() as block:
                    @block.sync
                    def _(sp):
                        load_group(sp, 0, 0, 0)
                        load_values(sp, 0, 0)
                        sp.wait_ge(stk0, LOADS)
                        sp.wait_ge(v_in0, 16)
                reset(sems)

                with nc.Fori(0, B // NB) as i_:
                    with nc.Block() as block:

                        @block.sync
                        def _(sp):
                            b0 = i_ * NB
                            load_group(sp, 1, b0, 1)
                            load_values(sp, 1, b0 + 1)
                            for q in range(2, NG + 1):
                                sp.wait_ge(full, (q - 1) * TG)
                                load_group(sp, q, (b0 + q // G) % B, q % G)
                                if q % G == 1:
                                    s = q // G - 1
                                    sp.wait_ge(weighed, (s + 1) * UN * KTU)
                                    load_values(sp, s + 2, (b0 + s + 2) % B)
                                    sp.wait_ge(fin, (s + 1) * UN)
                                    sp.dma_start(batch(o_dram, b0 + s).rearrange("a p s k n -> (a p) s k n"),
                                                 res_[:, s % 2]).then_inc(out_st[s % 2], 16)
                            sp.wait_ge(fin, NB * UN)
                            sp.dma_start(batch(o_dram, b0 + NB - 1).rearrange("a p s k n -> (a p) s k n"),
                                         res_[:, (NB - 1) % 2]).then_inc(out_st[(NB - 1) % 2], 16)
                            for s in range(2):
                                sp.wait_ge(stk[s], LOADS * (NG // 2))
                                sp.wait_ge(v_in[s], 16 * (NB // 2))
                                sp.wait_ge(out_st[s], 16 * (NB // 2))

                        @block.tensor
                        def _(pe):
                            def scores(i):
                                u, j, bb, g, t = place(i)
                                q = i // TG
                                if i % TG == 0 and q >= 1:
                                    pe.wait_ge(stk[q % 2], LOADS * ((q + 1) // 2))
                                if i >= 2:
                                    pe.wait_ge(nmx, i - 1)
                                for c in range(NC):
                                    last = nc.tensor.matmul(scores_ps[i % 2][:, c * CH:(c + 1) * CH],
                                                            stacks[:, q % 2, 0, j, t * P:(t + 1) * P],
                                                            stacks[:, q % 2, 1, j, c * CH:(c + 1) * CH], start=True, stop=True)
                                last.then_inc(full, 1)

                            def transposes(k):
                                u, kt = divmod(k, KTU)
                                if kt == 0:
                                    pe.wait_ge(exps, (u + 1) * HG)
                                if k >= 2:
                                    pe.wait_ge(tev[k % 2], k // 2)
                                for j in range(HG):
                                    last = nc.tensor.transpose(turned_ps[k % 2][:, j * P:(j + 1) * P],
                                                               ring[:, (u * HG + j) % PRING, kt * P:(kt + 1) * P], idf[:])
                                last.then_inc(t_full, 1)

                            def weigh(k):
                                u, kt = divmod(k, KTU)
                                _, _, bb, g, t = place(u * HG)
                                if k >= UN * KTU and k % (UN * KTU) == 0:
                                    pe.wait_ge(v_in[bb % 2], 16 * ((bb + 1) // 2))
                                pe.wait_ge(tev[k % 2], k // 2 + 1)
                                if kt == 0 and u >= 2:
                                    pe.wait_ge(of, u - 1)
                                for j in range(HG):
                                    last = nc.tensor.matmul(out_ps[u % 2][j * D:(j + 1) * D, 0:P],
                                                            V[:, bb % 2, kt, (g * HG + j) * D:(g * HG + j + 1) * D],
                                                            PTs[:, k % 3, j * P:(j + 1) * P],
                                                            start=(kt == 0), stop=(kt == KTU - 1), skip_group_check=True)
                                last.then_inc(weighed, 1)

                            def spread(u):
                                pe.wait_ge(rs, u + 1)
                                nc.tensor.matmul(out_ps[u % 2][:, P:2 * P], rsx[:, u % 2, :], idf[:], start=True,
                                                 stop=True).then_inc(spread_, 1)

                            scores(0)
                            for s in range(NTL + TLAG + 1):
                                for k in (2 * (s - TLAG), 2 * (s - TLAG) + 1):
                                    if 0 <= k < LK:
                                        transposes(k)
                                    if 0 <= k - 1 < LK:
                                        weigh(k - 1)
                                        if k % KTU == 0:
                                            spread(k // KTU - 1)
                                if s + 1 < NTL:
                                    scores(s + 1)

                        @block.scalar
                        def _(act):
                            def exponentials(i):
                                act.wait_ge(nmx, i + 1)
                                r = ring[:, i % PRING, :]
                                nc.scalar.activation(r, r, ACT.Exp, bias=nmax[:, i:i + 1], scale=-1.0,
                                                     accum_out=sums[:, i:i + 1]).then_inc(exps, 1)

                            def copy_out(k):
                                act.wait_ge(t_full, k + 1)
                                if k >= 3:
                                    act.wait_ge(weighed, k - 2)
                                nc.scalar.copy(PTs[:, k % 3, :], turned_ps[k % 2]).then_inc(ev_act, 1)

                            def copy_sums(u):
                                act.wait_ge(spread_, u + 1)
                                if u >= 2:
                                    act.wait_ge(of, u - 1)
                                nc.scalar.copy(rbs[:, u % 2, :], out_ps[u % 2][:, P:2 * P]).then_inc(rb_copy, 1)

                            for s in range(NTL + 2 * HG + 3):
                                if 1 <= s <= NTL:
                                    exponentials(s - 1)
                                k = 2 * (s - TLAG)
                                if 0 <= k < LK:
                                    copy_out(k)
                                v = s - 2 * HG - 2
                                if v >= 0 and v % HG == 0 and v // HG < NU:
                                    copy_sums(v // HG)

                        @block.gpsimd
                        def _(pool):
                            for u in range(NU):
                                _, _, bb, g, t = place(u * HG)
                                tok = slice(t * P, (t + 1) * P)
                                pool.wait_ge(of, u + 1)
                                if bb >= 2 and u % UN == 0:
                                    pool.wait_ge(out_st[bb % 2], 16 * (bb // 2))
                                nc.gpsimd.tensor_copy(res_[:, bb % 2, 0, g, tok], oF[:, u % 2, :]).then_inc(hi, 1)
                                pool.wait_ge(hi, u + 1)
                                nc.gpsimd.tensor_tensor(res_[:, bb % 2, 1, g, tok], oF[:, u % 2, :], res_[:, bb % 2, 0, g, tok],
                                                        ALU.subtract).then_inc(fin, 1)

                        @block.vector
                        def _(dve):
                            def row_max(i):
                                u, j, bb, g, t = place(i)
                                dve.wait_ge(full, i + 1)
                                if i >= PRING:
                                    dve.wait_ge(t_full, KTU * ((i - PRING) // HG + 1))
                                z = (ZU - W - ROWS * t) * W
                                nc.vector.tensor_tensor_reduce(
                                    out=ring[:, i % PRING, :], in0=scores_ps[i % 2], in1=bias[:, g * HG + j, z:z + N],
                                    scale=-1.0, scalar=3.0e38, op0=ALU.add, op1=ALU.min,
                                    accum_out=nmax[:, i:i + 1]).then_inc(nmx, 1)

                            def copy_out(k):
                                dve.wait_ge(t_full, k + 1)
                                if k >= 3:
                                    dve.wait_ge(weighed, k - 2)
                                nc.vector.tensor_copy(PTs[:, k % 3, :], turned_ps[k % 2]).then_inc(ev_dve, 1)

                            def reciprocals(u):
                                dve.wait_ge(exps, (u + 1) * HG)
                                nc.vector.reciprocal(rsum[:, u % 2, :], sums[:, u * HG:(u + 1) * HG]).then_inc(rs1, 1)
                                dve.wait_ge(rs1, u + 1)
                                if u >= 2:
                                    dve.wait_ge(spread_, u - 1)
                                nc.vector.tensor_copy(rsx[:, u % 2, :].rearrange("p (j d) -> p j d", j=HG),
                                                      rsum[:, u % 2, :].unsqueeze(2).broadcast_to([P, HG, D])).then_inc(rs, 1)

                            def finish(u):
                                _, _, bb, g, t = place(u * HG)
                                tok = slice(t * P, (t + 1) * P)
                                dve.wait_ge(rb_copy, u + 1)
                                dve.wait_ge(weighed, (u + 1) * KTU)
                                if u >= 2:
                                    dve.wait_ge(fin, u - 1)
                                nc.vector.tensor_tensor(oF[:, u % 2, :], out_ps[u % 2][:, 0:P], rbs[:, u % 2, :],
                                                        ALU.mult).then_inc(of, 1)

                            for s in range(NTL + 2 * HG + 4):
                                if s < NTL:
                                    row_max(s)
                                if s >= TLAG and (s - TLAG) % HG == 0 and (s - TLAG) // HG < NU:
                                    reciprocals((s - TLAG) // HG)
                                k = 2 * (s - TLAG) + 1
                                if 0 <= k < LK:
                                    copy_out(k)
                                v = s - 2 * HG - 3
                                if v >= 0 and v % HG == 0 and v // HG < NU:
                                    finish(v // HG)

                    reset(sems)

        def attention_keys_first():
            with ExitStack() as es:
                def ssem(name):
                    return es.enter_context(nc.semaphore(f"{name}_kf"))

                def tile(name, shape, dt):
                    return es.enter_context(nc.sbuf_tensor(f"{name}_kf", shape, dt))

                QHH, KHL, QL, KH1 = range(4)
                LEAD = 2 * D
                stacks = tile("stacks", [P, 2, 4, HG, N], F16)
                V = tile("V", [P, 2, NT, C], F32)
                res_ = tile("res", [P, 2, KT, N], F32)
                half_min = tile("half_min", [P, HG * TT, NC], F32)
                row_min = tile("row_min", [P, HG * TT], F32)
                max_row = tile("max_row", [HG * TT, 2, P], F16)
                PR = 4
                o1, o2 = HG * CH * PR, HG * CH * (PR + 2)
                prob = zf[:, 0:o1].rearrange("p (r j n) -> p r j n", r=PR, j=HG)
                acc = zf[:, o1:o2].rearrange("p (r j n) -> p r j n", r=2, j=HG)
                rec = zf[:, o2:o2 + CH]
                oS = zf[:, o2 + CH:o2 + 3 * CH].rearrange("p (r n) -> p r n", r=2)

                max_ps = [PS[:, i, :] for i in range(2)]
                score_ps = [PS[:, 2 + i, :] for i in range(3)]
                out_ps = [PS[:, 5 + i, :] for i in range(2)]
                den_ps = PS[:, 7, :]

                UB = G * NC
                NU = NB * UB
                NG = NB * G
                SU = KTU * HG
                NS_ = NU * SU
                MH = HG * TT * NC
                MJ = MH + 1
                PIECES = 4
                LOADS = 16 * 9
                ADDS = KTU - 1

                sems = [ssem(n) for n in ("stk0", "stk1", "v_in0", "v_in1", "x_in0", "x_in1", "out_st0", "out_st1", "m_in0",
                                          "m_in1", "emb_in", "fill", "max_full", "max_read", "min_ok", "full", "exps", "weighed",
                                          "acc_pool", "acc_dve", "den", "recd", "scaled", "fin")]
                (stk0, stk1, v_in0, v_in1, x_in0, x_in1, out_st0, out_st1, m_in0, m_in1, emb_in, fill, max_full, max_read, min_ok,
                 full, exps, weighed, acc_pool, acc_dve, den, recd, scaled, fin) = sems
                stk, v_in, x_in, out_st, m_in = (stk0, stk1), (v_in0, v_in1), (x_in0, x_in1), (out_st0, out_st1), (m_in0, m_in1)

                def load_group(sp, q, b, g):
                    src = batch(qk_dram[1], b)[:, g].rearrange("a s (j d) n -> d (a s) j n", d=D)
                    for r, st, s in ((0, QHH, 0), (1, QHH, 0), (2, QHH, 2), (3, QHH, 2), (0, KHL, 4), (1, KHL, 5),
                                     (0, QL, 1), (1, QL, 3), (0, KH1, 4)):
                        sp.dma_start(stacks[r * D:(r + 1) * D, q % 2, st], src[:, s]).then_inc(stk[q % 2], 16)

                def load_values(sp, n, b):
                    sp.dma_start(V[:, n % 2], batch(v_dram[1], b).rearrange("a p t c -> (a p) t c")).then_inc(v_in[n % 2], 16)

                def load_residual(sp, n, b):
                    sp.dma_start(res_[:, n % 2], batch(x1_dram, b).rearrange("a p k n -> (a p) k n")).then_inc(x_in[n % 2], 16)

                def queries(u):
                    return (u // NC) % G, (u % NC) * CH

                def move_maxima(sp, u, base):
                    slot, first = queries(u)
                    sp.wait_ge(max_read, base + MJ)
                    for j in range(HG):
                        sp.dma_start(stacks[LEAD:LEAD + 1, slot, QL, j, first:first + CH].rearrange("p (t n) -> p t n", n=P),
                                     max_row[j * TT:(j + 1) * TT, u % 2, :]).then_inc(m_in[u % 2], 16)

                def max_product(pe, u, base, m):
                    slot, first = queries(u)
                    n = base + m
                    if n >= 2:
                        pe.wait_ge(max_read, n - 1)
                    if m < MH:
                        i, c = divmod(m, NC)
                        j, t = divmod(i, TT)
                        nc.tensor.matmul(max_ps[n % 2], stacks[:, slot, QHH, j, first + t * P:first + (t + 1) * P],
                                         stacks[:, slot, KHL, j, c * CH:(c + 1) * CH], start=True,
                                         stop=True).then_inc(max_full, 1)
                    else:
                        pe.wait_ge(min_ok, base // MJ + 1)
                        nc.tensor.transpose(max_ps[n % 2][0:HG * TT, 0:P], row_min[:], idf[:]).then_inc(max_full, 1)

                def max_reduce(dve, u, base, m):
                    n = base + m
                    if m == MH:
                        dve.wait_ge(max_read, base + MH)
                        nc.vector.tensor_reduce(row_min[:], half_min[:], AX.X, ALU.min).then_inc(min_ok, 1)
                    dve.wait_ge(max_full, n + 1)
                    if m < MH:
                        i, c = divmod(m, NC)
                        nc.vector.tensor_reduce(half_min[:, i, c:c + 1], max_ps[n % 2], AX.X, ALU.min).then_inc(max_read, 1)
                    else:
                        nc.vector.tensor_scalar(max_row[:, u % 2, :], max_ps[n % 2][0:HG * TT, 0:P], -1.0, None,
                                                ALU.mult).then_inc(max_read, 1)

                with nc.Block() as block:
                    @block.sync
                    def _(sp):
                        for q in range(2):
                            sp.dma_start(stacks[2 * D:4 * D, q, KHL], edram.unsqueeze(1).broadcast_to([2 * D, HG, N])
                                         ).then_inc(emb_in, 16)
                            if q == 0:
                                load_group(sp, 0, 0, 0)
                        for q in range(2):
                            sp.dma_start(stacks[D:2 * D, q, KH1], edram[0:D, :].unsqueeze(1).broadcast_to([D, HG, N])
                                         ).then_inc(emb_in, 16)
                        load_values(sp, 0, 0)
                        sp.wait_ge(stk0, LOADS)
                        sp.wait_ge(v_in0, 16)
                        sp.wait_ge(fill, 6)
                        move_maxima(sp, 0, 0)
                        sp.wait_ge(m_in0, 16 * HG)

                    @block.tensor
                    def _(pe):
                        pe.wait_ge(emb_in, 16 * 4)
                        pe.wait_ge(stk0, LOADS)
                        for m in range(MJ):
                            max_product(pe, 0, 0, m)

                    @block.gpsimd
                    def _(pool):
                        for q in range(2):
                            nc.gpsimd.memset(stacks[LEAD:P, q, QL], 0.0).then_inc(fill, 1)
                            nc.gpsimd.memset(stacks[LEAD:P, q, KH1], 0.0).then_inc(fill, 1)
                            pool.wait_ge(fill, 3 * q + 2)
                            nc.gpsimd.memset(stacks[LEAD:LEAD + 1, q, KH1], 1.0).then_inc(fill, 1)

                    @block.vector
                    def _(dve):
                        for m in range(MJ):
                            max_reduce(dve, 0, 0, m)
                reset(sems)

                def max_jobs(s):
                    t, fast = s % SU, MAXIMA
                    if t < fast:
                        return range(MH * t // fast, MH * (t + 1) // fast)
                    return (MH,) if t == fast + 1 else ()

                MAXIMA, DEN, REC, SCALE = SU - 7, SU - 7, SU - 5, SU - 1

                with nc.Fori(0, B // NB) as i_:
                    with nc.Block() as block:

                        @block.sync
                        def _(sp):
                            b0 = i_ * NB
                            load_residual(sp, 0, b0)
                            for u in range(NU):
                                q, bb = u // NC, u // UB
                                if u % NC == 0:
                                    if q >= 1:
                                        sp.wait_ge(full, u * SU)
                                    load_group(sp, q + 1, (b0 + (q + 1) // G) % B, (q + 1) % G)
                                if u % UB == 0:
                                    if bb >= 1:
                                        sp.wait_ge(weighed, u * KTU)
                                    load_values(sp, bb + 1, (b0 + bb + 1) % B)
                                move_maxima(sp, u + 1, MJ * u)
                                if u % UB == 1:
                                    if bb >= 1:
                                        sp.wait_ge(fin, bb * UB)
                                        sp.dma_start(batch(t_dram, b0 + bb - 1).rearrange("a p k n -> (a p) k n"),
                                                     res_[:, (bb - 1) % 2]).then_inc(out_st[(bb - 1) % 2], 16)
                                        sp.wait_ge(out_st[(bb - 1) % 2], 16 * ((bb + 1) // 2))
                                    if bb + 1 < NB:
                                        load_residual(sp, bb + 1, b0 + bb + 1)
                            sp.wait_ge(fin, NU)
                            sp.dma_start(batch(t_dram, b0 + NB - 1).rearrange("a p k n -> (a p) k n"),
                                         res_[:, (NB - 1) % 2]).then_inc(out_st[(NB - 1) % 2], 16)
                            for n in range(2):
                                sp.wait_ge(out_st[n], 16 * (NB // 2))
                                sp.wait_ge(stk[n], LOADS * (NG // 2))
                                sp.wait_ge(v_in[n], 16 * (NB // 2))
                                sp.wait_ge(m_in[n], 16 * HG * (NU // 2))

                        @block.tensor
                        def _(pe):
                            def scores(s):
                                u, (kt, j) = s // SU, divmod(s % SU, HG)
                                slot, first = queries(u)
                                if s % SU == 0 and u >= 1:
                                    pe.wait_ge(m_in[u % 2], 16 * HG * ((u + 1) // 2))
                                if s >= 3:
                                    pe.wait_ge(exps, s - 2)
                                for n, (k_, q_) in enumerate(((KHL, QHH), (KH1, QL))):
                                    last = nc.tensor.matmul(score_ps[s % 3], stacks[:, slot, k_, j, kt * P:(kt + 1) * P],
                                                            stacks[:, slot, q_, j, first:first + CH], start=(n == 0), stop=(n == 1))
                                last.then_inc(full, 1)

                            def maxima(s):
                                u = s // SU
                                for m in max_jobs(s):
                                    if m == 0 and (u + 1) % NC == 0:
                                        q = (u + 1) // NC
                                        pe.wait_ge(stk[q % 2], LOADS * ((q + 1) // 2))
                                    max_product(pe, u + 1, MJ * u, m)

                            def weigh(n):
                                u, kt = divmod(n, KTU)
                                g, bb = (u // NC) % G, u // UB
                                if kt == 0 and u % UB == 0 and bb >= 1:
                                    pe.wait_ge(v_in[bb % 2], 16 * ((bb + 1) // 2))
                                if kt == 0 and u >= 2:
                                    pe.wait_ge(scaled, u - 1)
                                pe.wait_ge(exps, HG * (n + 1))
                                for j in range(HG):
                                    last = nc.tensor.matmul(out_ps[u % 2][j * D:(j + 1) * D, :],
                                                            V[:, bb % 2, kt, (g * HG + j) * D:(g * HG + j + 1) * D],
                                                            prob[:, n % PR, j, :], start=(kt == 0), stop=(kt == KTU - 1),
                                                            skip_group_check=True)
                                last.then_inc(weighed, 1)

                            def denominators(u):
                                pe.wait_ge(acc_pool, ADDS * (u + 1))
                                pe.wait_ge(acc_dve, ADDS * (u + 1))
                                if u >= 1:
                                    pe.wait_ge(recd, PIECES * u)
                                for j in range(HG):
                                    last = nc.tensor.matmul(den_ps[j * D:(j + 1) * D, :], ones[:, 0:D], acc[:, u % 2, j, :],
                                                            start=True, stop=True, skip_group_check=True)
                                last.then_inc(den, 1)

                            for s in range(NS_ + SU):
                                if s < NS_:
                                    scores(s)
                                    maxima(s)
                                n, r = divmod(s - HG - 2, HG)
                                if r == 0 and 0 <= n < NU * KTU:
                                    weigh(n)
                                if s >= SU and s % SU == DEN:
                                    denominators(s // SU - 1)

                        @block.scalar
                        def _(act):
                            for s in range(NS_):
                                n, j = divmod(s, HG)
                                if n >= PR and j in (0, HG - 1):
                                    u, kt = divmod(n - PR, KTU)
                                    if j == 0:
                                        act.wait_ge(weighed, n - PR + 1)
                                        act.wait_ge(acc_pool, ADDS * u + max(kt, 1))
                                    else:
                                        act.wait_ge(acc_dve, ADDS * u + max(kt, 1))
                                act.wait_ge(full, s + 1)
                                nc.scalar.activation(prob[:, n % PR, j, :], score_ps[s % 3], ACT.Exp,
                                                     scale=-1.0).then_inc(exps, 1)

                        def add_tile(eng, engine, n, heads, done):
                            u, kt = divmod(n, KTU)
                            if kt == 0:
                                return
                            engine.wait_ge(exps, HG * n + heads.stop)
                            if kt == 1 and u >= 2:
                                engine.wait_ge(den, u - 1)
                            if kt >= 2:
                                engine.wait_ge(done, ADDS * u + kt - 1)
                            so_far = prob[:, (n - 1) % PR, heads, :] if kt == 1 else acc[:, u % 2, heads, :]
                            eng.tensor_tensor(acc[:, u % 2, heads, :], so_far, prob[:, n % PR, heads, :],
                                              ALU.add).then_inc(done, 1)

                        @block.gpsimd
                        def _(pool):
                            def finish(u):
                                bb, g = u // UB, (u // NC) % G
                                _, first = queries(u)
                                pool.wait_ge(scaled, u + 1)
                                pool.wait_ge(x_in[bb % 2], 16 * (bb // 2 + 1))
                                r = res_[:, bb % 2, g, first:first + CH]
                                nc.gpsimd.tensor_tensor(r, r, oS[:, u % 2, :], ALU.add).then_inc(fin, 1)

                            for n in range(NU * KTU):
                                add_tile(nc.gpsimd, pool, n, slice(0, HG - 1), acc_pool)
                                if n % KTU == 0 and n >= 2 * KTU:
                                    finish(n // KTU - 2)
                            finish(NU - 2)
                            finish(NU - 1)

                        @block.vector
                        def _(dve):
                            def reciprocal(u, piece):
                                dve.wait_ge(den, u + 1)
                                if u >= 1:
                                    dve.wait_ge(scaled, u)
                                c = slice(piece * CH // PIECES, (piece + 1) * CH // PIECES)
                                nc.vector.reciprocal(rec[:, c], den_ps[:, c]).then_inc(recd, 1)

                            def scale_out(u):
                                dve.wait_ge(recd, PIECES * (u + 1))
                                dve.wait_ge(weighed, KTU * (u + 1))
                                if u >= 2:
                                    dve.wait_ge(fin, u - 1)
                                nc.vector.scalar_tensor_tensor(out=oS[:, u % 2, :], in0=out_ps[u % 2], scalar=1.0 / C,
                                                               in1=rec[:, :], op0=ALU.mult, op1=ALU.mult).then_inc(scaled, 1)

                            for s in range(NS_ + SU):
                                if s < NS_:
                                    for m in max_jobs(s):
                                        max_reduce(dve, s // SU + 1, MJ * (s // SU), m)
                                n, r = divmod(s - HG - 1, HG)
                                if r == 0 and 0 <= n < NU * KTU:
                                    add_tile(nc.vector, dve, n, slice(HG - 1, HG), acc_dve)
                                if s >= SU:
                                    u, t = s // SU - 1, s % SU
                                    if REC <= t < REC + PIECES:
                                        reciprocal(u, t - REC)
                                    if t == SCALE:
                                        scale_out(u)

                    reset(sems)

        token_phase(0)
        attention_queries_first()
        token_phase(1)
        attention_keys_first()
        token_phase(2)

        BE = B * E
        g4 = gates[:].rearrange("p (b t e) -> p b t e", b=B, t=NT)
        sc = sb("sink_scratch", [P, 9 * N], F32)[:, :]
        part = sc[:, 0:BE]
        rcp = sc[:, BE:2 * BE]
        gW = sc[0:BE, 2 * N:3 * N]
        top = sc[0:BE, 3 * N:3 * N + 8]
        mask = sc[:, 4 * N:4 * N + NT * BE]
        m4 = mask.rearrange("p (t b e) -> p b t e", t=NT, b=B)
        coef = sb("coef", [P, NT * BE], F32)[:, :]
        c4 = coef.rearrange("p (b t e) -> p b t e", b=B, t=NT)
        left = sc[:, 6 * N:6 * N + B * NT].rearrange("p (b t) -> p b t", b=B)
        tmp = sc[:, 7 * N:7 * N + B * NT].rearrange("p (b t) -> p b t", b=B)

        gT_src = sc[:, 8 * N:8 * N + NT * BE].rearrange("p (t c) -> p t c", t=NT)

        HB = sb("f_halves", [P, 2, 2, KT, N], F16)
        TB = sb("f_tokens", [P, 2, KT, N], F32)

        def load_tokens(sp, s, b, signal):
            sp.dma_start(HB[:, s], batch(h_dram, b).rearrange("a p s k n -> (a p) s k n")).then_inc(signal, 16)
            sp.dma_start(TB[:, s], batch(t_dram, b).rearrange("a p k n -> (a p) k n")).then_inc(signal, 16)

        zf16 = zf.bitcast(F16)
        ex_p = zf16[:, 0:2 * KT * E * C].rearrange("p (s k n) -> p s k n", s=2, k=KT)
        ex_f = zf[:, KT * E * C:2 * KT * E * C].rearrange("p (k n) -> p k n", k=KT)

        with ExitStack() as es:
            def ssem(name):
                return es.enter_context(nc.semaphore(name))
            prt, tot, g_t, g_w, m_t, ch, ex_in, ex_s, ex_h, first_in = (
                ssem(n) for n in ("prt", "tot", "g_t", "g_w", "m_t", "ch", "ex_in", "ex_s", "ex_h", "first_in"))
            blk = ExitStack()
            block = blk.enter_context(nc.Block())

            @block.sync
            def _(sp):
                for k in range(KT):
                    sp.dma_start(ex_f[:, k, :].rearrange("p (e o) -> p e o", e=E),
                                 experts[:, k * P:(k + 1) * P, :].rearrange("e p o -> p e o")).then_inc(ex_in, 16)
                load_tokens(sp, 0, 0, first_in)
                sp.wait_ge(first_in, 32)

            @block.scalar
            def _(act):
                for k in range(KT):
                    act.wait_ge(ex_in, 16 * KT)
                    nc.scalar.mul(ex_f[:, k, :], ex_f[:, k, :], WS).then_inc(ex_s, 1)
                for k in range(KT):
                    act.wait_ge(ex_s, k + 1)
                    nc.scalar.copy(ex_p[:, 0, k, :], ex_f[:, k, :]).then_inc(ex_h, 1)

            @block.gpsimd
            def _(pool):
                for k in range(KT):
                    pool.wait_ge(ex_h, k + 1)
                    nc.gpsimd.tensor_tensor(ex_p[:, 1, k, :], ex_f[:, k, :], ex_p[:, 0, k, :], ALU.subtract)

            @block.tensor
            def _(pe):
                for n in range(SINKHORN):
                    pe.wait_ge(prt, n + 1)
                    nc.tensor.matmul(PS[:, 2, 0:BE], ones[:], part, start=True, stop=True).then_inc(tot, 1)
                pe.wait_ge(g_t, 1)
                for t in range(NT):
                    last = nc.tensor.transpose(PS[0:BE, t // 4, (t % 4) * P:(t % 4 + 1) * P], gT_src[:, t, :], idf[:])
                last.then_inc(m_t, 1)
                pe.wait_ge(g_w, 1)
                for t in range(NT):
                    last = nc.tensor.transpose(PS[:, 3, t * BE:(t + 1) * BE], gW[:, t * P:(t + 1) * P], idf[0:BE, 0:BE])
                last.then_inc(m_t, 1)

            @block.vector
            def _(dve):
                chain = [0]

                def link(ins):
                    chain[0] += 1
                    ins.then_inc(ch, 1)
                    dve.wait_ge(ch, chain[0])

                p3 = part.rearrange("p (b e) -> p b e", b=B)
                r3 = rcp.rearrange("p (b e) -> p b e", b=B)
                rt = rcp.rearrange("p (b t) -> p b t", b=B)
                pt3 = part.rearrange("p (b t) -> p b t", b=B)
                for n in range(SINKHORN):
                    ins = nc.vector.reduce_sum(p3, g4.rearrange("p b t e -> p b e t"), AX.X)
                    ins.then_inc(prt, 1)
                    dve.wait_ge(tot, n + 1)
                    link(nc.vector.tensor_scalar(rcp, PS[:, 2, 0:BE], float(C), None, ALU.mult))
                    link(nc.vector.reciprocal(rcp, rcp))
                    link(nc.vector.tensor_tensor(g4, g4, r3.unsqueeze(2).broadcast_to([P, B, NT, E]), ALU.mult))
                    link(nc.vector.reduce_sum(pt3, g4, AX.X))
                    link(nc.vector.reciprocal(rt, pt3))
                    link(nc.vector.tensor_tensor(g4, g4, rt.unsqueeze(3).broadcast_to([P, B, NT, E]), ALU.mult))
                nc.vector.tensor_copy(gT_src.rearrange("p t (b e) -> p t b e", b=B),
                                      g4.rearrange("p b t e -> p t b e")).then_inc(g_t, 1)
                dve.wait_ge(m_t, 1)
                link(nc.vector.tensor_copy(gW.rearrange("p (a n) -> p a n", a=2), PS[0:BE, 0:2, :]))
                for r in range(M // 8):
                    link(nc.vector.max(top, gW))
                    link(nc.vector.match_replace(gW, top, gW, -1.0))
                ins = nc.vector.tensor_scalar(gW, gW, 0.0, None, ALU.is_lt)
                ins.then_inc(g_w, 1)
                dve.wait_ge(m_t, 2)
                link(nc.vector.tensor_copy(mask, PS[:, 3, :]))
                link(nc.vector.memset(left, 1.0))
                for e in reversed(range(E)):
                    link(nc.vector.tensor_tensor(tmp, m4[:, :, :, e], left, ALU.mult))
                    link(nc.vector.tensor_tensor(left, left, tmp, ALU.subtract))
                    link(nc.vector.tensor_tensor(c4[:, :, :, e], tmp, g4[:, :, :, e], ALU.mult))

            blk.close()
            reset([prt, tot, g_t, g_w, m_t, ch, ex_in, ex_s, ex_h, first_in])

        EJ = CH // C
        NJ = E // EJ
        FT = NB * NT
        cb = sb("f_coef", [P, NB * NT * E], F32)
        acc = sb("f_acc", [P, 2, C], F32)
        fsem = [sem(n) for n in ("f_in0", "f_in1", "f_full", "f_coef", "f_acc", "f_turned", "f_added", "f_out")]
        f_in0, f_in1, f_full, f_cf, f_acc, f_t, f_x, f_out = fsem
        f_in = (f_in0, f_in1)
        NPB = 6

        with nc.Fori(0, B // NB) as i_:
            with nc.Block() as block:

                @block.sync
                def _(sp):
                    b0 = i_ * NB
                    load_tokens(sp, 1, b0 + 1, f_in1)
                    for s in range(NB):
                        sp.wait_ge(f_x, (s + 1) * NT)
                        sp.dma_start(batch(out, b0 + s).rearrange("a (k p) n -> (a p) k n", p=P),
                                     TB[:, s % 2]).then_inc(f_out, 16)
                        sp.wait_ge(f_out, 16 * (s + 1))
                        if s + 2 <= NB:
                            load_tokens(sp, s % 2, (b0 + s + 2) % B, f_in[s % 2])
                    for s in range(2):
                        sp.wait_ge(f_in[s], 32 * (NB // 2))

                @block.tensor
                def _(pe):
                    def back(t):
                        pe.wait_ge(f_acc, (t + 1) * E)
                        if t >= 2:
                            pe.wait_ge(f_x, t - 1)
                        for k in range(KT):
                            last = nc.tensor.transpose(PS[:, NPB + t % 2, k * P:(k + 1) * P], acc[:, t % 2, k * P:(k + 1) * P], idf[:])
                        last.then_inc(f_t, 1)

                    for t in range(FT):
                        s_, tt = divmod(t, NT)
                        if tt == 0 and s_ >= 1:
                            pe.wait_ge(f_in[s_ % 2], 32 * ((s_ + 1) // 2))
                        for q in range(NJ):
                            n = t * NJ + q
                            if n >= NPB:
                                pe.wait_ge(f_acc, (n - NPB + 1) * EJ)
                            i = 0
                            for k in range(KT):
                                for s, w in ((0, 0), (0, 1), (1, 0)):
                                    last = nc.tensor.matmul(PS[:, n % NPB, :], HB[:, s_ % 2, s, k, tt * P:(tt + 1) * P],
                                                            ex_p[:, w, k, q * CH:(q + 1) * CH],
                                                            start=(i == 0), stop=(i == 3 * KT - 1))
                                    i += 1
                            last.then_inc(f_full, 1)
                            if q == 1 and t >= 1:
                                back(t - 1)
                    back(FT - 1)

                @block.vector
                def _(dve):
                    def add_back(t):
                        dve.wait_ge(f_t, t + 1)
                        s_, tt = divmod(t, NT)
                        if tt == 0 and s_ >= 1:
                            dve.wait_ge(f_in[s_ % 2], 32 * ((s_ + 1) // 2))
                        x_ = TB[:, s_ % 2, :, tt * P:(tt + 1) * P]
                        nc.vector.tensor_tensor(x_, x_, PS[:, NPB + t % 2, 0:C].rearrange("p (k n) -> p k n", k=KT),
                                                ALU.add).then_inc(f_x, 1)

                    nc.vector.tensor_scalar(cb[:], coef[:, bass.ds(i_ * (NB * NT * E), NB * NT * E)], 1.0 / WS, None,
                                            ALU.mult).then_inc(f_cf, 1)
                    dve.wait_ge(f_cf, 1)
                    for t in range(FT):
                        for e in range(E):
                            n = (t * E + e) // EJ
                            if e % EJ == 0:
                                dve.wait_ge(f_full, n + 1)
                            if e == 0 and t >= 2:
                                dve.wait_ge(f_t, t - 1)
                            ps = PS[:, n % NPB, (e % EJ) * C:(e % EJ + 1) * C]
                            c_e = cb[:, t * E + e:t * E + e + 1]
                            if e == 0:
                                ins = nc.vector.tensor_scalar(acc[:, t % 2, :], ps, c_e, None, ALU.mult)
                            else:
                                dve.wait_ge(f_acc, t * E + e)
                                ins = nc.vector.scalar_tensor_tensor(out=acc[:, t % 2, :], in0=ps, scalar=c_e,
                                                                     in1=acc[:, t % 2, :], op0=ALU.mult, op1=ALU.add)
                            ins.then_inc(f_acc, 1)
                            if e == 3 and t >= 1:
                                add_back(t - 1)
                    add_back(FT - 1)

            reset(fsem)


def kernel(**inputs):
    import numpy as np
    import concourse.bacc as _bacc
    from concourse import mybir as _mybir
    from concourse.bass_utils import run_bass_kernel_spmd as _run

    a = {k: np.asarray(v) for k, v in inputs.items()}
    B, C, HH, WW = a["x"].shape
    N, H = HH * WW, 8
    D = C // H
    con = np.ascontiguousarray
    wqkv = con(a["L0_conv_w_qkv"].T)
    wout = con(a["L0_conv_w_out"].T)
    w1 = a["L1_attn_W"].reshape(C, H, 3, D)
    b1 = a["L1_attn_b"].reshape(H, 3, D)
    swap = np.concatenate([np.arange(D // 2, D), np.arange(D // 2)])
    w1q = con(np.concatenate([w1[:, :, 0].reshape(C, C), w1[:, :, 0][:, :, swap].reshape(C, C),
                              w1[:, :, 1].reshape(C, C), w1[:, :, 2].reshape(C, C)], axis=1))
    cols = [b1[:, 0].reshape(-1, 128), b1[:, 0][:, swap].reshape(-1, 128), b1[:, 1].reshape(-1, 128)]
    b1cols = con(np.concatenate(cols, axis=0).T)
    b1v = con(b1[:, 2].reshape(-1))
    r = np.arange(-(WW - 1), WW, dtype=np.float32)
    lr = (-np.sign(r) * np.log(np.abs(r) + np.float32(1.0))).astype(np.float32)
    relt = con(np.stack([np.repeat(lr, len(r)), np.tile(lr, len(r))]))
    div = np.exp(-np.arange(0, D, 2, dtype=np.float32) * np.float32(np.log(10000.0) / D)).astype(np.float64)
    ang = div[:, None] * np.arange(N)[None, :]
    s, c = np.sin(ang), np.cos(ang)
    rot = np.stack([np.tile(np.concatenate([s, s]), (128 // D, 1)), np.tile(np.concatenate([c, -c]), (128 // D, 1))],
                   axis=1).astype(np.float32)
    etab = np.concatenate([c, s]).astype(np.float32)
    data = {
        "x": con(a["x"].reshape(B, C, N)),
        "gamma": con(a["L0_conv_gamma"].reshape(-1, 128).T),
        "wqkv": wqkv, "wout": wout, "w1q": w1q, "b1cols": b1cols, "b1v": b1v,
        "gatew": con(a["L1_ffn_gate_weight"][0]), "experts": con(a["L1_ffn_experts"]),
        "relt": relt,
        "cw0": con(a["L0_conv_cpb_w0"].T), "cb0": con(a["L0_conv_cpb_b0"][:, None]),
        "cw1": con(a["L0_conv_cpb_w1"].T), "cb1": con(a["L0_conv_cpb_b1"][:, None]),
        "cw2": con(a["L0_conv_cpb_w2"].T), "cb2": con(a["L0_conv_cpb_b2"][:, None]),
        "ident": np.eye(128, dtype=np.float32), "rot": con(rot), "etab": con(etab),
    }
    nc = _bacc.Bacc("TRN2", target_bir_lowering=False, num_devices=1)
    args = {k: nc.dram_tensor(f"in_{k}", list(v.shape), _mybir.dt.from_np(v.dtype), kind="ExternalInput").ap()
            for k, v in data.items()}
    out = nc.dram_tensor("out_0", [B, C, N], _mybir.dt.float32, kind="ExternalOutput").ap()
    build(nc, **args, out=out)
    res = _run(nc, [{f"in_{k}": v for k, v in data.items()}], core_ids=[0])
    return res.results[0]["out_0"].reshape(B, C, HH, WW)
```
